# Optimizing a Trainium2 kernel written in Bass

```python
import numpy as np
import jax
import jax.numpy as jnp

def _softmax(x, axis=-1):
    return jax.nn.softmax(x, axis=axis)

def _gelu(x):
    return jax.nn.gelu(x, approximate=True)

def _silu(x):
    return jax.nn.silu(x)

def _sigmoid(x):
    return jax.nn.sigmoid(x)

def _layernorm(x, axis=-1, eps=1e-05):
    m = jnp.mean(x, axis=axis, keepdims=True)
    v = jnp.var(x, axis=axis, keepdims=True)
    return (x - m) / jnp.sqrt(v + eps)

def _scatter_add(tgt, idx, src, axis=0):
    return tgt.at[idx].add(src)

def _segment_sum(src, seg, n):
    return jax.ops.segment_sum(src, seg, n)
kernel_name = 'mk_adj_ffn_d1_adj_r2_af4866'

def setup_inputs(seed: int=0):
    np.random.seed(seed)
    _w = jnp.asarray

    def _rec_inputs():
        import jax
        import jax.numpy as jnp
        _gk = jax.random.key(seed)
        x = -0.0005207 + 1.001 * jax.random.normal(jax.random.fold_in(_gk, 1), (4096, 128), jnp.float32)
        _w = (1.0 + jnp.arange(4096, dtype=jnp.float32)) ** (-0.5)
        _w = _w / _w.mean()
        _pij = jnp.clip(0.000488281 * _w[:, None] * _w[None, :], 0.0, 1.0)
        _a = jax.random.uniform(jax.random.fold_in(_gk, 2), (4096, 4096)) < _pij
        _a = jnp.logical_or(_a, jnp.eye(4096, dtype=bool))
        _af = _a.astype(jnp.float32)
        adj = _af
        return (x, adj)
    x, adj = _rec_inputs()

    def _L0_gnn_setup():
        import jax, jax.numpy as jnp
        import numpy as np
        N = 4096
        F = 128
        NEG_INF = -9000000000000000.0
        ALPHA = 0.2
        THRESH = 1e-06
        key = jax.random.key(seed)
        k1, k2, k3, k4 = jax.random.split(key, 4)
        x = jax.random.normal(k1, (N, F), jnp.float32)
        h0 = jax.random.normal(k2, (N, F), jnp.float32)
        limit = float(np.sqrt(6.0 / (2 * F + 1)) * 1.414)
        a = jax.random.uniform(k3, (2 * F, 1), jnp.float32, -limit, limit)
        temp = jnp.zeros((5,), jnp.float32)
        adj = jax.random.bernoulli(k4, 0.005, (N, N)).astype(jnp.float32)
        adj = jnp.maximum(adj, jnp.eye(N, dtype=jnp.float32))
        return {'x': x, 'h0': h0, 'a': a, 'temp': temp, 'adj': adj, 'l': 1}
    _L0_gnn_all = _L0_gnn_setup()
    _L0_gnn_in = {k: v for k, v in _L0_gnn_all.items() if k in ('h0', 'a', 'temp')}
    del _L0_gnn_all

    def _L0_ffn_setup():
        import jax, jax.numpy as jnp
        import numpy as np
        E = 8
        K = 2
        D = 128
        H = 256
        DOUT = 128
        EPS = 1e-05
        key = jax.random.key(seed)
        ks = jax.random.split(key, 9)
        s = 0.02
        return {'x': jax.random.normal(ks[0], (4, 4096, D), jnp.float32), 'gamma': 1.0 + 0.05 * jax.random.normal(ks[1], (D,), jnp.float32), 'beta': 0.05 * jax.random.normal(ks[2], (D,), jnp.float32), 'Wr': 0.01 * jax.random.normal(ks[3], (D, E), jnp.float32), 'br': jnp.zeros((E,), jnp.float32), 'W1': s * jax.random.normal(ks[4], (E, D, H), jnp.float32), 'b1': s * jax.random.normal(ks[5], (E, H), jnp.float32), 'W2': s * jax.random.normal(ks[6], (E, H, DOUT), jnp.float32), 'b2': s * jax.random.normal(ks[7], (E, DOUT), jnp.float32)}
    _L0_ffn_all = _L0_ffn_setup()
    _L0_ffn_in = {k: v for k, v in _L0_ffn_all.items() if k in ('gamma', 'beta', 'Wr', 'br', 'W1', 'b1', 'W2', 'b2')}
    del _L0_ffn_all
    return {'x': x, 'adj': adj, 'L0_gnn_h0': _L0_gnn_in['h0'], 'L0_gnn_a': _L0_gnn_in['a'], 'L0_gnn_temp': _L0_gnn_in['temp'], 'L0_ffn_gamma': _L0_ffn_in['gamma'], 'L0_ffn_beta': _L0_ffn_in['beta'], 'L0_ffn_Wr': _L0_ffn_in['Wr'], 'L0_ffn_br': _L0_ffn_in['br'], 'L0_ffn_W1': _L0_ffn_in['W1'], 'L0_ffn_b1': _L0_ffn_in['b1'], 'L0_ffn_W2': _L0_ffn_in['W2'], 'L0_ffn_b2': _L0_ffn_in['b2']}

def reference(x, adj, L0_gnn_h0, L0_gnn_a, L0_gnn_temp, L0_ffn_gamma, L0_ffn_beta, L0_ffn_Wr, L0_ffn_br, L0_ffn_W1, L0_ffn_b1, L0_ffn_W2, L0_ffn_b2):
    import jax
    import jax.numpy as jnp

    def _L0_gnn_ref(x, h0, a, temp, adj, l):
        import jax, jax.numpy as jnp
        import numpy as np
        N = 4096
        F = 128
        NEG_INF = -9000000000000000.0
        ALPHA = 0.2
        THRESH = 1e-06
        Fdim = x.shape[1]
        feat_1 = x @ a[:Fdim]
        feat_2 = x @ a[Fdim:]
        e = jax.nn.leaky_relu(feat_1 + feat_2.T, ALPHA)
        att = jnp.where(adj > 0, e, NEG_INF)
        U = jax.nn.softmax(att, axis=1)
        P = 0.5 * U
        prop_u = U @ x
        rowsum = jnp.sum(U * P, axis=1)
        coe = jax.nn.sigmoid(temp)
        xi = x * rowsum[:, None]
        feat_odd = prop_u - xi
        feat_even = x + prop_u - xi
        feat = coe[2] * feat_odd + (1.0 - coe[2]) * feat_even
        sgn = jnp.sign(feat)
        mod = jnp.abs(feat)
        mod = jnp.where(mod > THRESH, mod - THRESH, 0.0)
        feat = mod * sgn
        pu = U @ feat
        feat_odd2 = feat - coe[3] * pu
        feat_even2 = pu + feat_odd2 * rowsum[:, None]
        feat_odd2 = coe[0] * feat_odd2 + (1.0 - coe[0]) * h0
        out = coe[1] * feat_even2 + (1.0 - coe[1]) * feat_odd2
        return out

    def _L0_ffn_ref(x, gamma, beta, Wr, br, W1, b1, W2, b2):
        import jax, jax.numpy as jnp
        import numpy as np
        E = 8
        K = 2
        D = 128
        H = 256
        DOUT = 128
        EPS = 1e-05
        mu = jnp.mean(x, axis=-1, keepdims=True)
        var = jnp.mean(jnp.square(x - mu), axis=-1, keepdims=True)
        xn = (x - mu) * jax.lax.rsqrt(var + EPS) * gamma + beta
        logits = jnp.einsum('bsd,de->bse', xn, Wr) + br
        top_vals, top_idx = jax.lax.top_k(logits, K)
        w = jax.nn.softmax(top_vals, axis=-1)
        w_full = jnp.einsum('bsk,bske->bse', w, jax.nn.one_hot(top_idx, E, dtype=w.dtype))
        y = jnp.zeros(x.shape[:-1] + (DOUT,), x.dtype)
        for e in range(E):
            h = jax.nn.gelu(jnp.einsum('bsd,dh->bsh', xn, W1[e]) + b1[e], approximate=False)
            y_e = jnp.einsum('bsh,hd->bsd', h, W2[e]) + b2[e]
            y = y + y_e * w_full[..., e, None]
        return y
    x = x + _L0_gnn_ref(_layernorm(x, axis=-1), L0_gnn_h0, L0_gnn_a, L0_gnn_temp, adj, 1)
    x = x + _L0_ffn_ref(_layernorm(x, axis=-1)[None], L0_ffn_gamma, L0_ffn_beta, L0_ffn_Wr, L0_ffn_br, L0_ffn_W1, L0_ffn_b1, L0_ffn_W2, L0_ffn_b2)[0]
    return x

_drawn_inputs = setup_inputs


def setup_inputs(seed=0):
    import zlib

    import numpy as np

    out = dict(_drawn_inputs(seed))
    spreads = {'L0_gnn_temp': (0.0, 0.8), 'L0_ffn_br': (0.0, 0.434)}
    factors = {'L0_ffn_gamma': 8.0,
     'L0_ffn_beta': 8.0,
     'L0_ffn_Wr': 5.628,
     'L0_ffn_W1': 3.663,
     'L0_ffn_b1': 8.0,
     'L0_ffn_W2': 3.604,
     'L0_ffn_b2': 7.002}
    for name, (base, spread) in spreads.items():
        noise = np.random.default_rng([zlib.crc32(name.encode()), seed]).standard_normal(out[name].shape)
        drawn = base * np.exp(spread * noise) if base else spread * noise
        out[name] = jnp.asarray(drawn.astype(out[name].dtype))
    for name, factor in factors.items():
        out[name] = (out[name] * factor).astype(out[name].dtype)
    return out
```

```python
from contextlib import ExitStack

import concourse.bass as bass
from concourse import mybir

P = 128
N = 4096
F = 128
T = N // P
SB = 4
W = SB * P
S = T // SB
CH = 4
JB = 2 * CH
B = T // JB
E = 8
H = 256
HH = H // P
EPS = 1e-5
THRESH = 1e-6
HEADROOM = 60.0
VS = 512.0
QS = 2.0 ** -60

F32 = mybir.dt.float32
BF16 = mybir.dt.bfloat16
F16 = mybir.dt.float16
U8 = mybir.dt.uint8
U32 = mybir.dt.uint32
ALU = mybir.AluOpType
ACT = mybir.ActivationFunctionType
X = mybir.AxisListType.X


def program(nc, x, adj, h0, a, temp, gamma, beta, Wr, br, W1, b1, W2, b2, out):
    with ExitStack() as ctx:
        def sb(name, shape, dt=F32):
            return ctx.enter_context(nc.sbuf_tensor(name, shape, dt))

        def sem(name):
            return ctx.enter_context(nc.semaphore(name))

        ds = bass.ds
        feat_dram = nc.dram_tensor("feat_dram", (N, F), F32, kind="Internal").ap()
        thr_dram = nc.dram_tensor("thr_dram", (T, P), F32, kind="Internal").ap()

        edges = sb("edges", [P, T * N], U8)
        stage = sb("stage", [P, 4096])
        nat = sb("nat", [P, 2048])
        thr = sb("thr", [P, 2, W])
        v = sb("v", [P, 2, T, 2 * F], F16)
        sq = sb("sq", [P, T, 2, 6], BF16)
        ring = sb("ring", [P, 2, 4, W], BF16)
        t1 = sb("t1", [P, SB, 2 * F])
        xs = sb("xs", [P, SB, F])
        colmean = sb("colmean", [P, F])
        identb = sb("identb", [P, P], BF16)
        ident = sb("ident", [P, P])
        mean = sb("mean", [P, T])
        rstd = sb("rstd", [P, T])
        kpow = sb("kpow", [P, 3, T])
        mant = sb("mant", [P, 2, T])
        wts = sb("wts", [P, T, 4])
        cc = sb("cc", [P, T, 3])
        rs = sb("rs", [P, T])
        coe = sb("coe", [P, 12])
        f2 = sb("f2", [P, T])
        meancol = sb("meancol", [P, 1])
        loc = sb("loc", [P, 16, SB])
        small = sb("small", [P, 6, 8])
        pro = edges[:, 0:4 * 16384].bitcast(F32)
        xn = pro[:, 0:4096].rearrange("p (t d) -> p t d", d=F)
        tmpa = pro[:, 4096:8192].rearrange("p (t d) -> p t d", d=F)
        tmpb = pro[:, 8192:12288].rearrange("p (t d) -> p t d", d=F)
        ab = pro[:, 12288:12544].rearrange("p (k d) -> p k d", d=F)
        pf = pro[:, 12544:13568].rearrange("p (k t) -> p k t", t=T)
        gmax = pro[:, 13696:13698]
        thrT = pro[0:T, 13824:13952]
        adjc = stage[:].rearrange("p (c t w) -> p c t w", c=2, t=SB)
        natb = nat[:].bitcast(BF16).rearrange("p (c t w) -> p c t w", c=2, t=SB)
        feats = stage[:].rearrange("p (t d) -> p t d", d=F)
        w1s = stage[:, 0:2048].rearrange("p (e h) -> p e h", e=E)
        w2s = stage[:, 2048:4096].rearrange("p (e k d) -> p e k d", e=E, k=HH)
        hT = nat[:, 0:1024].rearrange("p (k w) -> p k w", k=HH)
        ft = nat[:, 1024:1536].rearrange("p (t d) -> p t d", d=F)
        h0s = nat[:, 1536:2048].rearrange("p (t d) -> p t d", d=F)
        xnT = thr[:, 0, :]
        prod = thr[:, 1, :]
        wrs = sb("wrs", [P, E])
        b2s = sb("b2s", [E, F])
        bcol = sb("bcol", [P, E, HH])
        gb = sb("gb", [P, 2])
        brb = sb("brb", [P, E])
        iota = sb("iota", [P, E])
        lg = sb("lg", [P, SB, E])
        top = sb("top", [P, SB, 8])
        tix = sb("tix", [P, SB, 8], U32)
        wf = sb("wf", [P, 2, SB, E])
        wT = thr[0:E, 1, :]

        bank = [ctx.enter_context(nc.psum_tensor(f"bank{i}", [P, 512], F32)) for i in range(8)]
        acc, sqb = bank[0:4], bank[4]
        tp = [bank[5], bank[6]]
        hb = [bank[5], bank[6]]
        yb = [bank[4], bank[7]]

        x_in, a_in, w_in, wl_in = sem("x_in"), sem("a_in"), sem("w_in"), sem("wl_in")
        const_done = sem("const_done")
        adj_in = [sem("adj_in0"), sem("adj_in1")]
        ln_done, sq_done = sem("ln_done"), sem("sq_done")
        pro_dve, pro_act, pro_pe = sem("pro_dve"), sem("pro_act"), sem("pro_pe")
        thr_out, thr_in, thr_free = sem("thr_out"), sem("thr_in"), sem("thr_free")
        v_done = sem("v_done")
        gt_done, tp_done, code_done = sem("gt_done"), sem("tp_done"), sem("code_done")
        pos_ready, neg_ready, ring_free = sem("pos_ready"), sem("neg_ready"), sem("ring_free")
        scale_ready, evac_done, acc_free = sem("scale_ready"), sem("evac_done"), sem("acc_free")
        xs_in, feat_ready, feat_out = sem("xs_in"), sem("feat_ready"), sem("feat_out")
        feat_turn = sem("feat_turn")
        f_in, v2_done, weights_in = sem("f_in"), sem("v2_done"), sem("weights_in")
        mean_done = sem("mean_done")
        x2_in, ln2_var, ln2_sqrt, xn2_ready = sem("x2_in"), sem("ln2_var"), sem("ln2_sqrt"), sem("xn2_ready")
        xT_done, xT_ready, lg_done, gap_ready, gap_exp = (
            sem("xT_done"), sem("xT_ready"), sem("lg_done"), sem("gap_ready"), sem("gap_exp"))
        wf_ready, wT_done, wT_ready, b2_done, b2_added = (
            sem("wf_ready"), sem("wT_done"), sem("wT_ready"), sem("b2_done"), sem("b2_added"))
        h_done, h_ready, y_done, y_added = sem("h_done"), sem("h_ready"), sem("y_done"), sem("y_added")
        out_ready, out_done, x_used, t1_free = sem("out_ready"), sem("out_done"), sem("x_used"), sem("t1_free")

        adj_v = adj.rearrange("(t p) (k w) -> p t k w", p=P, w=CH * P)
        x_v = x.rearrange("(t p) d -> p t d", p=P)
        h0_v = h0.rearrange("(t p) d -> p t d", p=P)
        out_v = out.rearrange("(t p) d -> p t d", p=P)
        feat_v = feat_dram.rearrange("(t p) d -> p t d", p=P)
        PAIRS = T // 2
        BP = JB // 2

        def row(ap, n):
            return ap.rearrange("(o n) -> o n", o=1).to_broadcast([P, n])

        block = ctx.enter_context(nc.Block())

        @block.sync
        def _(sp):
            sp.dma_start(xn, x_v).then_inc(x_in, 16)
            for k in range(2):
                sp.dma_start(ab[:, k, :], row(a[k * F:(k + 1) * F, :].rearrange("f o -> (f o)"), F)).then_inc(a_in, 16)
            sp.dma_start(coe[:, 0:5], row(temp, 5)).then_inc(a_in, 16)

            def chunk(s, b, c):
                sp.dma_start(adjc[:, c], adj_v[:, ds(s * SB, SB), b * 2 + c, :]).then_inc(adj_in[c], 16)

            chunk(0, 0, 0)
            chunk(0, 0, 1)
            sp.wait_ge(pro_act, 4)
            sp.dma_start(thr_dram, thrT).then_inc(thr_out, 16)
            sp.wait_ge(thr_out, 16)

            def superblock(s, b0):
                for b in range(b0, B):
                    for c in range(2):
                        sp.wait_ge(gt_done, s * (2 * B) + (2 * b + c - 1))
                        sp.dma_start(adjc[:, c], adj_v[:, ds(s * SB, SB), b * 2 + c, :]).then_inc(adj_in[c], 16)

            superblock(0, 1)
            with sp.Fori(1, S, 1) as s:
                superblock(s, 0)

            sp.wait_ge(feat_out, 16 * S)
            sp.wait_ge(gt_done, 2 * B * S)
            sp.dma_start(feats, feat_v).then_inc(f_in, 16)
            sp.wait_ge(v2_done, S)
            sp.wait_ge(mean_done, 1)
            sp.dma_start(w1s, W1.rearrange("e d h -> d e h")).then_inc(weights_in, 16)
            sp.dma_start(w2s, W2.rearrange("e (k h) d -> h e k d", h=P)).then_inc(weights_in, 16)
            sp.sem_inc(t1_free, 1)
            with sp.Fori(0, S, 1) as s:
                sp.wait_ge(out_ready, s + 1)
                sp.dma_start(out_v[:, ds(s * SB, SB), :], t1[:, :, F:2 * F]).then_inc(out_done, 16)
                sp.wait_ge(out_done, s * 16 + 16)
                sp.sem_inc(t1_free, 1)
            sp.wait_ge(out_done, 16 * S)

        @block.gpsimd
        def _(pool):
            nc.gpsimd.memset(identb[:], 0.0)
            nc.gpsimd.memset(ident[:], 0.0)
            nc.gpsimd.memset(meancol[:], 1.0 / N)
            nc.gpsimd.iota(iota[:], [[1, E]], base=0, channel_multiplier=0,
                           allow_small_or_imprecise_dtypes=True)
            pool.drain()
            nc.gpsimd.affine_select(out=identb[:], in_=identb[:], compare_op=ALU.not_equal, fill=1.0,
                                    base=0, pattern=[[-1, P]], channel_multiplier=1)
            nc.gpsimd.affine_select(out=ident[:], in_=ident[:], compare_op=ALU.not_equal, fill=1.0,
                                    base=0, pattern=[[-1, P]], channel_multiplier=1)
            pool.drain().then_inc(const_done, 1)
            pool.dma_start(wrs[:], Wr).then_inc(w_in, 16)
            pool.dma_start(b2s[:], b2).then_inc(w_in, 16)
            pool.dma_start(gb[:, 0:1], gamma.rearrange("(d o) -> d o", o=1)).then_inc(w_in, 16)
            pool.dma_start(gb[:, 1:2], beta.rearrange("(d o) -> d o", o=1)).then_inc(w_in, 16)
            pool.dma_start(brb[:], row(br, E)).then_inc(w_in, 16)
            with nc.allow_non_contiguous_dma(reason="8 KiB of biases, once"):
                pool.dma_start(bcol[:], b1.rearrange("e (k h) -> h e k", h=P)).then_inc(w_in, 16)
            pool.wait_ge(pro_dve, 1)
            nc.gpsimd.partition_all_reduce(gmax[:, 1:2], gmax[:, 0:1], P,
                                           bass.bass_isa.ReduceOp.max).then_inc(pro_dve, 1)
            pool.wait_ge(thr_out, 16)

            def inputs(s, first):
                if not first:
                    pool.wait_ge(thr_free, s)
                    pool.wait_ge(thr_out, 16)
                pool.dma_start(thr[:, 0, :].rearrange("p (t d) -> p t d", d=P),
                               thr_dram[ds(s * SB, SB), :].unsqueeze(0).to_broadcast([P, SB, P])
                               ).then_inc(thr_in, 16)
                pool.dma_start(xs[:], x_v[:, ds(s * SB, SB), :]).then_inc(xs_in, 16)
                pool.wait_ge(feat_ready, s + 1)
                pool.sem_inc(feat_turn, 1)
                pool.dma_start(feat_v[:, ds(s * SB, SB), :], xs[:]).then_inc(feat_out, 16)
                pool.wait_ge(feat_out, s * 16 + 16)

            inputs(0, True)
            with pool.Fori(1, S, 1) as s:
                inputs(s, False)

            pool.wait_ge(v2_done, S)

            def inputs2(s, first):
                if not first:
                    pool.wait_ge(x_used, s)
                    pool.wait_ge(v2_done, S)
                pool.dma_start(xs[:], x_v[:, ds(s * SB, SB), :]).then_inc(x2_in, 16)
                pool.dma_start(h0s, h0_v[:, ds(s * SB, SB), :]).then_inc(x2_in, 16)
                pool.dma_start(ft, feat_v[:, ds(s * SB, SB), :]).then_inc(x2_in, 16)

            inputs2(0, True)
            with pool.Fori(1, S, 1) as s:
                inputs2(s, False)

        @block.scalar
        def _(act):
            act.wait_ge(ln_done, 1)
            nc.scalar.activation(tmpa, xn, ACT.Square).then_inc(sq_done, 1)
            act.wait_ge(ln_done, 2)
            nc.scalar.activation(rstd[:], pf[:, 0], ACT.Sqrt).then_inc(sq_done, 1)
            act.wait_ge(a_in, 48)
            nc.scalar.activation(coe[:, 5:10], coe[:, 0:5], ACT.Exp, scale=-1.0).then_inc(pro_act, 1)
            act.wait_ge(pro_dve, 3)
            nc.scalar.activation(pf[:, 8:12], pf[:, 4:8], ACT.Exp).then_inc(pro_act, 1)
            act.wait_ge(pro_pe, 1)
            nc.scalar.activation(thrT, bank[7][0:T, 0:P], ACT.Copy).then_inc(pro_act, 2)
            act.wait_ge(pro_dve, 4)

            def evacuate(s, scaled):
                act.wait_ge(scale_ready, scaled)
                for t in range(SB):
                    nc.scalar.activation(t1[:, t, :], acc[t][:, 0:2 * F], ACT.Copy,
                                         scale=loc[:, 0, t:t + 1]).then_inc(evac_done, 1)

            def positive_masks(s, b, n, coded):
                for q in range(JB):
                    if q % 2 == 0:
                        if not coded:
                            act.wait_ge(code_done, n * BP + (q // 2 + 1))
                        act.wait_ge(ring_free, n * BP + (q // 2 + 1))
                    jt = b * JB + q
                    ins = nc.scalar.activation(ring[:, 0, q % 4, :], edges[:, ds(jt * N + s * W, W)], ACT.Relu,
                                               bias=kpow[:, 1, ds(jt, 1)], scale=kpow[:, 0, ds(jt, 1)])
                    if q % 2:
                        ins.then_inc(pos_ready, 1)

            with act.Fori(0, S, 1) as s:
                with act.Fori(0, B, 1) as b:
                    positive_masks(s, b, s * B + b, False)
                evacuate(s, s + 1)

            with act.Fori(0, S, 1) as s:
                with act.Fori(0, B, 1) as b:
                    positive_masks(s, b, (s + S) * B + b, True)
                evacuate(s, s + (S + 1))
                act.wait_ge(ln2_var, s + 1)
                nc.scalar.activation(loc[:, 8, :], loc[:, 7, :], ACT.Sqrt).then_inc(ln2_sqrt, 1)
                act.wait_ge(gap_ready, s + 1)
                nc.scalar.activation(small[:, 1, 0:SB], small[:, 0, 0:SB], ACT.Exp).then_inc(gap_exp, 1)
                for e in range(E):
                    for k in range(HH):
                        act.wait_ge(h_done, s * (E * HH) + (e * HH + k + 1))
                        if k == 0:
                            act.wait_ge(y_done, s * E + (e + 1))
                        nc.scalar.activation(hT[:, k, :], hb[k][:], ACT.Gelu,
                                             bias=bcol[:, e, k:k + 1]).then_inc(h_ready, 1)

        @block.vector
        def _(dve):
            def bc(ap, n=T):
                return ap.unsqueeze(2).to_broadcast([P, n, F])

            dve.wait_ge(x_in, 16)
            nc.vector.tensor_reduce(mean[:], xn, X, ALU.add)
            dve.drain()
            nc.vector.tensor_scalar(mean[:], mean[:], 1.0 / F, None, ALU.mult)
            dve.drain()
            nc.vector.tensor_tensor(xn, xn, bc(mean[:]), ALU.subtract).then_inc(ln_done, 1)
            dve.wait_ge(sq_done, 1)
            nc.vector.tensor_reduce(pf[:, 0], tmpa, X, ALU.add)
            dve.drain()
            nc.vector.tensor_scalar(pf[:, 0], pf[:, 0], 1.0 / F, EPS, ALU.mult, ALU.add).then_inc(ln_done, 1)
            dve.wait_ge(sq_done, 2)
            nc.vector.reciprocal(rstd[:], rstd[:])
            dve.drain()
            nc.vector.tensor_tensor(xn, xn, bc(rstd[:]), ALU.mult)
            dve.wait_ge(a_in, 48)
            dve.drain()
            nc.vector.tensor_tensor(tmpa, xn, ab[:, 0, :].unsqueeze(1).to_broadcast([P, T, F]), ALU.mult)
            nc.vector.tensor_tensor(tmpb, xn, ab[:, 1, :].unsqueeze(1).to_broadcast([P, T, F]), ALU.mult)
            dve.drain().then_inc(ln_done, 1)
            nc.vector.tensor_reduce(pf[:, 1], tmpa, X, ALU.add)
            nc.vector.tensor_reduce(pf[:, 2], tmpb, X, ALU.add)
            dve.drain()
            nc.vector.tensor_scalar(pf[:, 3], pf[:, 1], -1.0, None, ALU.mult).then_inc(ln_done, 1)
            nc.vector.tensor_reduce(gmax[:, 0:1], pf[:, 2], X, ALU.max).then_inc(pro_dve, 1)
            dve.wait_ge(pro_act, 1)
            nc.vector.tensor_scalar(coe[:, 5:10], coe[:, 5:10], 1.0, None, ALU.add)
            dve.drain()
            nc.vector.reciprocal(coe[:, 0:5], coe[:, 5:10])
            dve.drain()
            nc.vector.tensor_scalar(coe[:, 5:10], coe[:, 0:5], -1.0, 1.0, ALU.mult, ALU.add)
            dve.drain()
            nc.vector.tensor_tensor(coe[:, 10:11], coe[:, 6:7], coe[:, 0:1], ALU.mult)
            nc.vector.tensor_tensor(coe[:, 11:12], coe[:, 6:7], coe[:, 5:6], ALU.mult)
            nc.vector.tensor_scalar(coe[:, 8:9], coe[:, 3:4], -1.0, None, ALU.mult)
            dve.wait_ge(pro_dve, 2)
            nc.vector.tensor_scalar(pf[:, 4], pf[:, 2], gmax[:, 1:2], None, ALU.subtract)
            nc.vector.tensor_scalar(pf[:, 6], pf[:, 1], gmax[:, 1:2], None, ALU.add)
            dve.drain()
            nc.vector.tensor_scalar(pf[:, 5], pf[:, 4], 0.2, HEADROOM, ALU.mult, ALU.add)
            nc.vector.tensor_scalar(pf[:, 7], pf[:, 6], 0.2, None, ALU.mult)
            dve.drain()
            nc.vector.tensor_scalar(pf[:, 4], pf[:, 4], HEADROOM, None, ALU.add)
            nc.vector.tensor_tensor(pf[:, 12], pf[:, 6], pf[:, 7], ALU.max)
            dve.drain()
            nc.vector.tensor_tensor(pf[:, 6], pf[:, 6], pf[:, 12], ALU.subtract)
            nc.vector.tensor_tensor(pf[:, 7], pf[:, 7], pf[:, 12], ALU.subtract)
            dve.drain().then_inc(pro_dve, 1)
            dve.wait_ge(pro_act, 2)
            fac = pf[:, 8:10].bitcast(U32)
            nc.vector.tensor_scalar(pf[:, 13:15].bitcast(U32), fac, 0x7F800000, None, ALU.bitwise_and)
            nc.vector.tensor_scalar(pf[:, 15:17].bitcast(U32), fac, 0x007FFFFF, 0x3F800000,
                                    ALU.bitwise_and, ALU.bitwise_or)
            dve.drain()
            nc.vector.tensor_copy(kpow[:, 0], pf[:, 13])
            nc.vector.tensor_scalar(kpow[:, 1], pf[:, 13], -2.0, None, ALU.mult)
            nc.vector.tensor_copy(kpow[:, 2], pf[:, 14])
            nc.vector.tensor_scalar(mant[:], pf[:, 15:17], VS, None, ALU.mult)
            sqv = sq[:].rearrange("p t g (k c) -> p g t k c", k=2)
            nc.vector.tensor_tensor(pf[:, 17:19], pf[:, 15:17], pf[:, 15:17], ALU.mult)
            nc.vector.tensor_scalar(pf[:, 19:21], pf[:, 13:15], QS, None, ALU.mult)
            dve.drain()
            nc.vector.tensor_tensor(pf[:, 17:19], pf[:, 17:19], pf[:, 19:21], ALU.mult)
            dve.drain()
            for k, src in enumerate((pf[:, 15:17], pf[:, 17:19])):
                for c in range(3):
                    nc.vector.tensor_copy(sqv[:, :, :, k, c], src)
                    dve.drain()
                    if c < 2:
                        nc.vector.tensor_tensor(src, src, sqv[:, :, :, k, c], ALU.subtract)
                        dve.drain()
            nc.vector.tensor_copy(wts[:, :, 0], pf[:, 10])
            nc.vector.tensor_copy(wts[:, :, 2], pf[:, 11])
            nc.vector.tensor_tensor(wts[:, :, 1], pf[:, 10], pf[:, 10], ALU.mult)
            nc.vector.tensor_tensor(wts[:, :, 3], pf[:, 11], pf[:, 11], ALU.mult)
            dve.wait_ge(pro_pe, 2)
            nc.vector.tensor_copy(colmean[:], bank[6][:, 0:F])

            def split(src, g, t0, n, scratch):
                nc.vector.tensor_tensor(scratch, src, bc(mant[:, g, t0:t0 + n], n), ALU.mult)
                dve.drain()
                nc.vector.tensor_copy(v[:, g, t0:t0 + n, 0:F], scratch)
                dve.drain()
                return nc.vector.tensor_tensor(v[:, g, t0:t0 + n, F:2 * F], scratch,
                                               v[:, g, t0:t0 + n, 0:F], ALU.subtract)

            split(xn, 0, 0, T, tmpa)
            split(xn, 1, 0, T, tmpb)
            dve.drain().then_inc(v_done, 1)

            def zero_two(c, landed):
                dve.wait_ge(adj_in[c], landed)
                nc.vector.tensor_scalar(natb[:, c], adjc[:, c], 0.0, 2.0, ALU.is_gt, ALU.mult).then_inc(gt_done, 1)

            def codes(s, b, n, p):
                dve.wait_ge(tp_done, n * BP + (p + 1))
                for q in (2 * p, 2 * p + 1):
                    jt = b * JB + q
                    ins = nc.vector.scalar_tensor_tensor(
                        edges[:, ds(jt * N + s * W, W)], thr[:, 1, :], f2[:, ds(jt, 1)],
                        tp[p % 2][:].bitcast(BF16)[:, (q % 2) * W:(q % 2 + 1) * W], ALU.is_lt, ALU.add)
                ins.then_inc(code_done, 1)

            def negative_masks(s, b, n, p, copied):
                dve.wait_ge(ring_free, n * BP + (p + 1))
                if copied:
                    dve.wait_ge(code_done, n * BP + (p + 1))
                for q in (2 * p, 2 * p + 1):
                    jt = b * JB + q
                    ins = nc.vector.tensor_scalar(ring[:, 1, q % 4, :], edges[:, ds(jt * N + s * W, W)], 2.0,
                                                  kpow[:, 2, ds(jt, 1)], ALU.is_equal, ALU.mult)
                ins.then_inc(neg_ready, 1)

            nc.vector.tensor_copy(f2[:], pf[:, 2])
            dve.drain().then_inc(pro_dve, 1)

            def step(s, b, n, last=False):
                zero_two(1, n * 16 + 16)
                for p in range(BP):
                    if p == BP // 2 and not last:
                        zero_two(0, n * 16 + 32)
                    codes(s, b, n, p)
                    negative_masks(s, b, n, p, True)

            def combine(evacuated):
                for t in range(SB):
                    dve.wait_ge(evac_done, evacuated + (t + 1))
                    nc.vector.scalar_tensor_tensor(t1[:, t, :], acc[t][:, 2 * F:4 * F], loc[:, 1, t:t + 1],
                                                   t1[:, t, :], ALU.mult, ALU.add).then_inc(acc_free, 1)
                dve.drain()
                nc.vector.tensor_tensor(t1[:, :, 0:F], t1[:, :, 0:F], t1[:, :, F:2 * F], ALU.add)
                dve.drain()

            def add_empty(flag):
                nc.vector.tensor_tensor(t1[:, :, F:2 * F], colmean[:].unsqueeze(1).to_broadcast([P, SB, F]),
                                        bc(flag, SB), ALU.mult)
                dve.drain()
                nc.vector.tensor_tensor(t1[:, :, 0:F], t1[:, :, 0:F], t1[:, :, F:2 * F], ALU.add)
                dve.drain()

            def rows1(s):
                sl = ds(s * SB, SB)
                dve.wait_ge(ring_free, s * PAIRS + (PAIRS + 2))
                nc.vector.tensor_reduce(loc[:, 2:6].rearrange("p k t -> p (k t)"),
                                        sqb[:, 0:SB * 12].rearrange("p (g c) -> p g c", c=3), X, ALU.add)
                dve.drain()
                sums = loc[:, 2:6].rearrange("p k t -> p (k t)").rearrange("p (t g) -> p t g", g=4)
                nc.vector.tensor_tensor(sums, sums, wts[:, sl, :], ALU.mult)
                dve.drain()
                nc.vector.tensor_tensor(sums[:, :, 0:2], sums[:, :, 0:2], sums[:, :, 2:4], ALU.add)
                dve.drain()
                nc.vector.tensor_scalar(loc[:, 6], sums[:, :, 0], 0.0, None, ALU.is_equal)
                dve.drain()
                nc.vector.tensor_tensor(loc[:, 7], sums[:, :, 0], loc[:, 6], ALU.add)
                dve.drain()
                nc.vector.reciprocal(loc[:, 8], loc[:, 7])
                dve.drain()
                nc.vector.tensor_scalar(loc[:, 9], loc[:, 8], 1.0 / VS, None, ALU.mult)
                nc.vector.tensor_tensor(loc[:, 10], sums[:, :, 1], loc[:, 8], ALU.mult)
                dve.drain()
                nc.vector.tensor_tensor(loc[:, 0], loc[:, 9], wts[:, sl, 0], ALU.mult)
                nc.vector.tensor_tensor(loc[:, 1], loc[:, 9], wts[:, sl, 2], ALU.mult)
                dve.drain().then_inc(scale_ready, 1)
                nc.vector.tensor_copy(cc[:, sl, 0], loc[:, 0])
                nc.vector.tensor_copy(cc[:, sl, 1], loc[:, 1])
                nc.vector.tensor_copy(cc[:, sl, 2], loc[:, 6])
                nc.vector.scalar_tensor_tensor(loc[:, 11], loc[:, 10], 0.5 / QS, loc[:, 8], ALU.mult, ALU.mult)
                dve.drain()
                nc.vector.scalar_tensor_tensor(loc[:, 12], loc[:, 6], 0.5 / N, loc[:, 11], ALU.mult, ALU.add)
                dve.drain()
                nc.vector.tensor_copy(rs[:, sl], loc[:, 12])
                nc.vector.tensor_scalar(loc[:, 13], loc[:, 12], -1.0, coe[:, 7:8], ALU.mult, ALU.add)
                dve.drain()
                nc.vector.tensor_tensor(loc[:, 14], loc[:, 13], rstd[:, sl], ALU.mult)
                combine(s * SB)
                dve.wait_ge(xs_in, s * 16 + 16)
                nc.vector.tensor_tensor(xs[:], xs[:], bc(mean[:, sl], SB), ALU.subtract)
                add_empty(loc[:, 6])
                nc.vector.tensor_tensor(xs[:], xs[:], bc(loc[:, 14], SB), ALU.mult)
                dve.drain()
                nc.vector.tensor_tensor(xs[:], xs[:], t1[:, :, 0:F], ALU.add)
                dve.drain()
                nc.vector.tensor_scalar(t1[:, :, 0:F], xs[:], -THRESH, THRESH, ALU.max, ALU.min)
                dve.drain()
                nc.vector.tensor_tensor(xs[:], xs[:], t1[:, :, 0:F], ALU.subtract).then_inc(feat_ready, 1)

            def superblock(s, last=False):
                dve.wait_ge(thr_in, s * 16 + 16)
                nc.vector.tensor_copy(thr[:, 1, :], thr[:, 0, :])
                dve.drain().then_inc(thr_free, 1)
                step(s, 0, s * B)
                with dve.Fori(1, B - 1 if last else B, 1) as b:
                    step(s, b, s * B + b)
                if last:
                    step(s, B - 1, s * B + (B - 1), last=True)
                rows1(s)

            zero_two(0, 16)
            with dve.Fori(0, S - 1, 1) as s:
                superblock(s)
            superblock(S - 1, last=True)

            dve.wait_ge(ring_free, S * PAIRS + 2)
            dve.wait_ge(f_in, 16)
            for g in range(S):
                src = feats[:, g * SB:(g + 1) * SB]
                pr = prod.rearrange("p (t d) -> p t d", d=F)
                split(src, 0, g * SB, SB, pr)
                dve.drain()
                split(src, 1, g * SB, SB, pr)
                dve.drain().then_inc(v2_done, 1)
            dve.wait_ge(mean_done, 1)
            nc.vector.tensor_copy(colmean[:], bank[7][:, 0:F])
            dve.wait_ge(w_in, 96)

            def rows2(s):
                sl = ds(s * SB, SB)
                dve.wait_ge(t1_free, s + 1)
                dve.wait_ge(ring_free, (s + S) * PAIRS + (PAIRS + 2))
                nc.vector.tensor_copy(loc[:, 0], cc[:, sl, 0])
                nc.vector.tensor_copy(loc[:, 1], cc[:, sl, 1])
                nc.vector.tensor_copy(loc[:, 6], cc[:, sl, 2])
                dve.drain().then_inc(scale_ready, 1)
                nc.vector.tensor_scalar(loc[:, 2], rs[:, sl], coe[:, 1:2], coe[:, 10:11], ALU.mult, ALU.add)
                combine((s + S) * SB)
                add_empty(loc[:, 6])
                dve.wait_ge(x2_in, s * 48 + 48)
                pu = t1[:, :, 0:F]
                nc.vector.scalar_tensor_tensor(ft, pu, coe[:, 8:9], ft, ALU.mult, ALU.add)
                nc.vector.scalar_tensor_tensor(xs[:], pu, coe[:, 1:2], xs[:], ALU.mult, ALU.add)
                dve.drain()
                nc.vector.scalar_tensor_tensor(xs[:], h0s, coe[:, 11:12], xs[:], ALU.mult, ALU.add)
                nc.vector.tensor_tensor(ft, ft, bc(loc[:, 2], SB), ALU.mult)
                dve.drain()
                x2 = t1[:, :, F:2 * F]
                nc.vector.tensor_tensor(x2, xs[:], ft, ALU.add)
                dve.drain().then_inc(x_used, 1)
                for t in range(SB):
                    nc.vector.bn_stats(small[:, 2 + t, 0:6], x2[:, t, :])
                dve.drain()
                for t in range(SB):
                    nc.vector.bn_aggr(loc[:, 9:11, t], small[:, 2 + t, 0:6])
                dve.drain()
                nc.vector.tensor_scalar(loc[:, 11], loc[:, 10], EPS, EPS, ALU.add, ALU.mult)
                dve.drain()
                nc.vector.tensor_tensor(loc[:, 7], loc[:, 11], loc[:, 10], ALU.add).then_inc(ln2_var, 1)
                dve.wait_ge(ln2_sqrt, s + 1)
                nc.vector.reciprocal(loc[:, 12], loc[:, 8])
                dve.drain()
                for t in range(SB):
                    ins = nc.vector.tensor_scalar(t1[:, t, 0:F], x2[:, t, :], loc[:, 9, t:t + 1],
                                                  loc[:, 12, t:t + 1], ALU.subtract, ALU.mult)
                ins.then_inc(xn2_ready, 1)
                dve.wait_ge(xT_done, s + 1)
                nc.vector.tensor_scalar(xnT, hb[0][:], gb[:, 0:1], gb[:, 1:2], ALU.mult, ALU.add).then_inc(xT_ready, 1)
                dve.wait_ge(lg_done, s + 1)
                nc.vector.tensor_tensor(lg[:], hb[1][:, 0:SB * E].rearrange("p (t e) -> p t e", e=E),
                                        brb[:].unsqueeze(1).to_broadcast([P, SB, E]), ALU.add)
                dve.drain()
                for t in range(SB):
                    nc.vector.max(top[:, t, :], lg[:, t, :])
                dve.drain()
                for t in range(SB):
                    nc.vector.max_index(tix[:, t, :], top[:, t, :], lg[:, t, :])
                nc.vector.tensor_tensor(small[:, 0, 0:SB], top[:, :, 1], top[:, :, 0], ALU.subtract).then_inc(gap_ready, 1)
                dve.drain()
                nc.vector.tensor_copy(top[:, :, 2:4], tix[:, :, 0:2])
                dve.wait_ge(gap_exp, s + 1)
                nc.vector.tensor_scalar(loc[:, 13], small[:, 1, 0:SB], 1.0, None, ALU.add)
                dve.drain()
                nc.vector.reciprocal(loc[:, 14], loc[:, 13])
                dve.drain()
                nc.vector.tensor_tensor(loc[:, 15], loc[:, 14], small[:, 1, 0:SB], ALU.mult)
                dve.drain()
                for t in range(SB):
                    for k in range(2):
                        nc.vector.tensor_scalar(wf[:, k, t, :], iota[:], top[:, t, 2 + k:3 + k],
                                                loc[:, 14 + k, t:t + 1], ALU.is_equal, ALU.mult)
                dve.drain()
                nc.vector.tensor_tensor(wf[:, 0], wf[:, 0], wf[:, 1], ALU.add).then_inc(wf_ready, 1)
                dve.wait_ge(wT_done, s + 1)
                nc.vector.tensor_copy(wT, yb[1][0:E, :]).then_inc(wT_ready, 1)
                dve.wait_ge(b2_done, s + 1)
                nc.vector.tensor_tensor(x2, x2, yb[0][:].rearrange("p (t d) -> p t d", d=F), ALU.add).then_inc(b2_added, 1)
                for e in range(E):
                    dve.drain()
                    dve.wait_ge(y_done, s * E + (e + 2))
                    for t in range(SB):
                        ins = nc.vector.scalar_tensor_tensor(
                            x2[:, t, :], yb[(e + 1) % 2][:, t * F:(t + 1) * F], wf[:, 0, t, e:e + 1],
                            x2[:, t, :], ALU.mult, ALU.add)
                    ins.then_inc(y_added, 1)
                dve.drain().then_inc(out_ready, 1)

            with dve.Fori(0, S, 1) as s:
                with dve.Fori(0, B, 1) as b:
                    for p in range(BP):
                        negative_masks(s, b, (s + S) * B + b, p, False)
                rows2(s)

        @block.tensor
        def _(pe):
            pe.sem_inc(ring_free, 2)
            pe.sem_inc(acc_free, SB)
            pe.wait_ge(const_done, 1)
            pe.wait_ge(ln_done, 4)
            nc.tensor.transpose(bank[7][0:T, 0:P], pf[:, 3], ident[:]).then_inc(pro_pe, 1)
            for t in range(T):
                mm = nc.tensor.matmul(bank[6][:, 0:F], meancol[:].to_broadcast([P, P]), xn[:, t, :], start=(t == 0), stop=(t == T - 1))
            mm.then_inc(pro_pe, 1)
            pe.wait_ge(v_done, 1)

            def turn(p, chunks):
                pe.wait_ge(gt_done, chunks)
                for q in range(2):
                    for t in range(SB):
                        k = (2 * p + q) % CH
                        tr = nc.tensor.transpose(
                            tp[p % 2][:].bitcast(BF16)[:, q * W + t * P:q * W + (t + 1) * P],
                            natb[:, (p * 2) // CH % 2, t, k * P:(k + 1) * P], identb[:])
                tr.then_inc(tp_done, 1)

            def sums(b, n, p, first, with_squares):
                pe.wait_ge(pos_ready, n * BP + (p + 1))
                pe.wait_ge(neg_ready, n * BP + (p + 1))
                for q in (2 * p, 2 * p + 1):
                    jt = b * JB + q
                    lead = first and q == 0
                    for t in range(SB):
                        for g in range(2):
                            lhs = ring[:, g, q % 4, t * P:(t + 1) * P]
                            mm = nc.tensor.matmul(acc[t][:, g * 2 * F:(g + 1) * 2 * F], lhs, v[:, g, jt, :],
                                                  start=lead and g == 0, stop=False, skip_group_check=True)
                            if with_squares:
                                o = (t * 2 + g) * 6
                                mm = nc.tensor.matmul(sqb[:, o:o + 6], lhs, sq[:, jt, g, :],
                                                      start=lead and g == 0 and t == 0, stop=False,
                                                      skip_group_check=True)
                mm.then_inc(ring_free, 1)

            def step(s, b, first=False, last=False):
                n = s * B + b
                for p in range(BP):
                    sums(b, n, p, first, True)
                    if p < BP - 2 or not last:
                        turn((p + 2) % BP, n * 2 + ((p + 2) // 2 + 1))

            def superblock(s, last=False):
                pe.wait_ge(acc_free, s * SB + SB)
                step(s, 0, first=True)
                with pe.Fori(1, B - 1 if last else B, 1) as b:
                    step(s, b)
                if last:
                    step(s, B - 1, last=True)

            turn(0, 1)
            turn(1, 1)
            with pe.Fori(0, S - 1, 1) as s:
                superblock(s)
            superblock(S - 1, last=True)

            pe.wait_ge(f_in, 16)
            for t in range(T):
                mm = nc.tensor.matmul(bank[7][:, 0:F], meancol[:].to_broadcast([P, P]), feats[:, t, :], start=(t == 0), stop=(t == T - 1))
            mm.then_inc(mean_done, 1)
            pe.wait_ge(v2_done, S)
            pe.wait_ge(w_in, 96)
            pe.wait_ge(weights_in, 32)
            pe.sem_inc(y_done, 1)
            pe.sem_inc(y_added, 1)

            with pe.Fori(0, S, 1) as s:
                pe.wait_ge(acc_free, s * SB + (S * SB + SB))
                for p in range(BP):
                    sums(0, (s + S) * B, p, True, False)
                with pe.Fori(1, B, 1) as b:
                    for p in range(BP):
                        sums(b, (s + S) * B + b, p, False, False)
                pe.wait_ge(xn2_ready, s + 1)
                pe.wait_ge(y_added, s * E + 1)
                for t in range(SB):
                    tr = nc.tensor.transpose(hb[0][:, t * P:(t + 1) * P], t1[:, t, 0:F], ident[:])
                tr.then_inc(xT_done, 1)
                pe.wait_ge(xT_ready, s + 1)
                for t in range(SB):
                    mm = nc.tensor.matmul(hb[1][:, t * E:(t + 1) * E], xnT[:, t * P:(t + 1) * P], wrs[:],
                                          start=True, stop=True)
                mm.then_inc(lg_done, 1)
                pe.wait_ge(wf_ready, s + 1)
                for t in range(SB):
                    tr = nc.tensor.transpose(yb[1][0:E, t * P:(t + 1) * P], wf[:, 0, t, :], ident[:])
                tr.then_inc(wT_done, 1)
                pe.wait_ge(wT_ready, s + 1)
                for t in range(SB):
                    mm = nc.tensor.matmul(yb[0][:, t * F:(t + 1) * F], wT[:, t * P:(t + 1) * P], b2s[:],
                                          start=True, stop=True)
                mm.then_inc(b2_done, 1)

                def hidden(e):
                    for k in range(HH):
                        if e:
                            pe.wait_ge(h_ready, s * (E * HH) + (e * HH + k - 1))
                        nc.tensor.matmul(hb[k][:], w1s[:, e, k * P:(k + 1) * P], xnT,
                                         start=True, stop=True).then_inc(h_done, 1)

                hidden(0)
                for e in range(E):
                    pe.wait_ge(h_ready, s * (E * HH) + (e * HH + 2))
                    if e + 1 < E:
                        hidden(e + 1)
                    pe.wait_ge(y_added, s * E + max(e, 1))
                    if e == 1:
                        pe.wait_ge(b2_added, s + 1)
                    for t in range(SB):
                        for k in range(HH):
                            mm = nc.tensor.matmul(yb[(e + 1) % 2][:, t * F:(t + 1) * F],
                                                  hT[:, k, t * P:(t + 1) * P], w2s[:, e, k, :],
                                                  start=(k == 0), stop=(k == HH - 1))
                    mm.then_inc(y_done, 1)


_INS = ["x", "adj", "L0_gnn_h0", "L0_gnn_a", "L0_gnn_temp", "L0_ffn_gamma", "L0_ffn_beta", "L0_ffn_Wr",
        "L0_ffn_br", "L0_ffn_W1", "L0_ffn_b1", "L0_ffn_W2", "L0_ffn_b2"]


def kernel(**inputs):
    import numpy as _np
    import concourse.bacc as _bacc
    from concourse import mybir as _mybir
    from concourse.bass_utils import run_bass_kernel_spmd as _run

    nc = _bacc.Bacc("TRN2", target_bir_lowering=False, num_devices=1)
    arrays, args = {}, []
    for name in _INS:
        arr = _np.ascontiguousarray(inputs[name])
        arrays[f"in_{name}"] = arr
        args.append(nc.dram_tensor(f"in_{name}", arr.shape, _mybir.dt.from_np(arr.dtype), kind="ExternalInput").ap())
    args.append(nc.dram_tensor("out_x", (N, F), F32, kind="ExternalOutput").ap())
    program(nc, *args)
    r = _run(nc, [arrays], core_ids=[0])
    return r.results[0]["out_x"]
```

```python
from contextlib import ExitStack

import concourse.bass as bass
from concourse import mybir

P = 128
N = 4096
F = 128
T = N // P
SB = 4
W = SB * P
S = T // SB
CH = 4
JB = 2 * CH
B = T // JB
E = 8
H = 256
HH = H // P
EPS = 1e-5
THRESH = 1e-6
HEADROOM = 60.0
VS = 512.0
QS = 2.0 ** -60

F32 = mybir.dt.float32
BF16 = mybir.dt.bfloat16
F16 = mybir.dt.float16
U8 = mybir.dt.uint8
U32 = mybir.dt.uint32
ALU = mybir.AluOpType
ACT = mybir.ActivationFunctionType
X = mybir.AxisListType.X


def program(nc, x, adj, h0, a, temp, gamma, beta, Wr, br, W1, b1, W2, b2, out):
    with ExitStack() as ctx:
        def sb(name, shape, dt=F32):
            return ctx.enter_context(nc.sbuf_tensor(name, shape, dt))

        def sem(name):
            return ctx.enter_context(nc.semaphore(name))

        ds = bass.ds
        feat_dram = nc.dram_tensor("feat_dram", (N, F), F32, kind="Internal").ap()
        thr_dram = nc.dram_tensor("thr_dram", (T, P), F32, kind="Internal").ap()

        edges = sb("edges", [P, T * N], U8)
        stage = sb("stage", [P, 4096])
        nat = sb("nat", [P, 2048])
        thr = sb("thr", [P, 2, W])
        v = sb("v", [P, 2, T, 2 * F], F16)
        sq = sb("sq", [P, T, 2, 6], BF16)
        ring = sb("ring", [P, 2, 4, W], BF16)
        t1 = sb("t1", [P, SB, 2 * F])
        xs = sb("xs", [P, SB, F])
        colmean = sb("colmean", [P, F])
        identb = sb("identb", [P, P], BF16)
        ident = sb("ident", [P, P])
        mean = sb("mean", [P, T])
        rstd = sb("rstd", [P, T])
        kpow = sb("kpow", [P, 3, T])
        mant = sb("mant", [P, 2, T])
        wts = sb("wts", [P, T, 4])
        cc = sb("cc", [P, T, 3])
        rs = sb("rs", [P, T])
        coe = sb("coe", [P, 12])
        f2 = sb("f2", [P, T])
        meancol = sb("meancol", [P, 1])
        loc = sb("loc", [P, 16, SB])
        small = sb("small", [P, 6, 8])
        pro = edges[:, 0:4 * 16384].bitcast(F32)
        xn = pro[:, 0:4096].rearrange("p (t d) -> p t d", d=F)
        tmpa = pro[:, 4096:8192].rearrange("p (t d) -> p t d", d=F)
        tmpb = pro[:, 8192:12288].rearrange("p (t d) -> p t d", d=F)
        ab = pro[:, 12288:12544].rearrange("p (k d) -> p k d", d=F)
        pf = pro[:, 12544:13568].rearrange("p (k t) -> p k t", t=T)
        gmax = pro[:, 13696:13698]
        thrT = pro[0:T, 13824:13952]
        adjc = stage[:].rearrange("p (c t w) -> p c t w", c=2, t=SB)
        natb = nat[:].bitcast(BF16).rearrange("p (c t w) -> p c t w", c=2, t=SB)
        feats = stage[:].rearrange("p (t d) -> p t d", d=F)
        w1s = stage[:, 0:2048].rearrange("p (e h) -> p e h", e=E)
        w2s = stage[:, 2048:4096].rearrange("p (e k d) -> p e k d", e=E, k=HH)
        hT = [nat[:, 0:1024].rearrange("p (k w) -> p k w", k=HH),
              sb("hT1", [P, HH, W])]
        x2 = sb("x2", [P, SB, F])
        ft = nat[:, 1024:1536].rearrange("p (t d) -> p t d", d=F)
        h0s = nat[:, 1536:2048].rearrange("p (t d) -> p t d", d=F)
        xnT = thr[:, 0, :]
        prod = thr[:, 1, :]
        wrs = sb("wrs", [P, E])
        b2s = sb("b2s", [E, F])
        bcol = sb("bcol", [P, E, HH])
        gb = sb("gb", [P, 2])
        brb = sb("brb", [P, E])
        iota = sb("iota", [P, E])
        lg = sb("lg", [P, SB, E])
        top = sb("top", [P, SB, 8])
        tix = sb("tix", [P, SB, 8], U32)
        wf = sb("wf", [P, 2, SB, E])
        wT = thr[0:E, 1, :]

        bank = [ctx.enter_context(nc.psum_tensor(f"bank{i}", [P, 512], F32)) for i in range(8)]
        acc, sqb = bank[0:4], bank[4]
        tp = [bank[5], bank[6]]
        hb = [bank[5], bank[6]]
        yb = [bank[4], bank[7]]

        x_in, a_in, w_in, wl_in = sem("x_in"), sem("a_in"), sem("w_in"), sem("wl_in")
        const_done = sem("const_done")
        adj_in = [sem("adj_in0"), sem("adj_in1")]
        ln_done, sq_done = sem("ln_done"), sem("sq_done")
        pro_dve, pro_act, pro_pe = sem("pro_dve"), sem("pro_act"), sem("pro_pe")
        thr_out, thr_in, thr_free = sem("thr_out"), sem("thr_in"), sem("thr_free")
        v_done = sem("v_done")
        gt_done, tp_done, code_done = sem("gt_done"), sem("tp_done"), sem("code_done")
        pos_ready, neg_ready, ring_free = sem("pos_ready"), sem("neg_ready"), sem("ring_free")
        scale_ready, evac_done, acc_free = sem("scale_ready"), sem("evac_done"), sem("acc_free")
        xs_in, feat_ready, feat_out = sem("xs_in"), sem("feat_ready"), sem("feat_out")
        xn_ready, rows_ready = sem("xn_ready"), sem("rows_ready")
        f_in, v2_done, weights_in = sem("f_in"), sem("v2_done"), sem("weights_in")
        mean_done = sem("mean_done")
        x2_in, ln2_var, ln2_sqrt, xn2_ready = sem("x2_in"), sem("ln2_var"), sem("ln2_sqrt"), sem("xn2_ready")
        xT_done, xT_ready, lg_done, gap_ready, gap_exp = (
            sem("xT_done"), sem("xT_ready"), sem("lg_done"), sem("gap_ready"), sem("gap_exp"))
        wf_ready, wT_done, wT_ready, b2_done, b2_added = (
            sem("wf_ready"), sem("wT_done"), sem("wT_ready"), sem("b2_done"), sem("b2_added"))
        h_done, h_ready, y_done, y_added = sem("h_done"), sem("h_ready"), sem("y_done"), sem("y_added")
        out_ready, out_done, x_used, x2_free = sem("out_ready"), sem("out_done"), sem("x_used"), sem("x2_free")

        adj_v = adj.rearrange("(t p) (k w) -> p t k w", p=P, w=CH * P)
        x_v = x.rearrange("(t p) d -> p t d", p=P)
        h0_v = h0.rearrange("(t p) d -> p t d", p=P)
        out_v = out.rearrange("(t p) d -> p t d", p=P)
        feat_v = feat_dram.rearrange("(t p) d -> p t d", p=P)
        RING = 4
        PAIRS = T // 2
        BP = JB // 2

        FE = 4

        def row(ap, n):
            return ap.rearrange("(o n) -> o n", o=1).to_broadcast([P, n])

        block = ctx.enter_context(nc.Block())

        @block.sync
        def _(sp):
            sp.dma_start(xn, x_v).then_inc(x_in, 16)
            for k in range(2):
                sp.dma_start(ab[:, k, :], row(a[k * F:(k + 1) * F, :].rearrange("f o -> (f o)"), F)).then_inc(a_in, 16)
            sp.dma_start(coe[:, 0:5], row(temp, 5)).then_inc(a_in, 16)

            def chunk(s, b, c):
                sp.dma_start(adjc[:, c], adj_v[:, ds(s * SB, SB), b * 2 + c, :]).then_inc(adj_in[c], 16)

            def next_chunks(s, b):
                for c in range(2):
                    sp.wait_ge(gt_done, s * (2 * B) + (2 * b + c - 1))
                    chunk(s, b, c)

            def thresholds(s):
                sp.dma_start(thr[:, 0, :].rearrange("p (t d) -> p t d", d=P),
                             thr_dram[ds(s * SB, SB), :].unsqueeze(0).to_broadcast([P, SB, P])
                             ).then_inc(thr_in, 16)

            def rows(s):
                sp.dma_start(xs[:], x_v[:, ds(s * SB, SB), :]).then_inc(xs_in, 16)

            def store_features(s):
                sp.wait_ge(feat_ready, s + 1)
                sp.dma_start(feat_v[:, ds(s * SB, SB), :], xs[:]).then_inc(feat_out, 16)

            def superblock(s, first=False, last=False):
                if not first:
                    next_chunks(s, 0)
                next_chunks(s, 1)
                if not last:
                    sp.wait_ge(thr_free, s + 1)
                    thresholds(s + 1)
                next_chunks(s, 2)
                if not first:
                    store_features(s - 1)
                next_chunks(s, 3)
                if not first:
                    sp.wait_ge(feat_out, s * 16)
                    rows(s)

            chunk(0, 0, 0)
            chunk(0, 0, 1)
            sp.wait_ge(pro_act, 4)
            sp.dma_start(thr_dram, thrT).then_inc(thr_out, 16)
            sp.wait_ge(thr_out, 16)
            thresholds(0)
            rows(0)
            superblock(0, first=True)
            with sp.Fori(1, S - 1, 1) as s:
                superblock(s)
            superblock(S - 1, last=True)
            store_features(S - 1)

            sp.wait_ge(feat_out, 16 * S)
            sp.wait_ge(gt_done, 2 * B * S)
            sp.dma_start(feats, feat_v).then_inc(f_in, 16)
            sp.wait_ge(v2_done, S)
            sp.wait_ge(mean_done, 1)
            sp.dma_start(w1s, W1.rearrange("e d h -> d e h")).then_inc(weights_in, 16)
            sp.dma_start(w2s, W2.rearrange("e (k h) d -> h e k d", h=P)).then_inc(weights_in, 16)
            sp.sem_inc(x2_free, 1)
            with sp.Fori(0, S, 1) as s:
                sp.wait_ge(out_ready, s + 1)
                sp.dma_start(out_v[:, ds(s * SB, SB), :], x2[:]).then_inc(out_done, 16)
                sp.wait_ge(out_done, s * 16 + 16)
                sp.sem_inc(x2_free, 1)
            sp.wait_ge(out_done, 16 * S)

        @block.gpsimd
        def _(pool):
            nc.gpsimd.memset(identb[:], 0.0)
            nc.gpsimd.memset(ident[:], 0.0)
            nc.gpsimd.memset(meancol[:], 1.0 / N)
            nc.gpsimd.iota(iota[:], [[1, E]], base=0, channel_multiplier=0,
                           allow_small_or_imprecise_dtypes=True)
            pool.drain()
            nc.gpsimd.affine_select(out=identb[:], in_=identb[:], compare_op=ALU.not_equal, fill=1.0,
                                    base=0, pattern=[[-1, P]], channel_multiplier=1)
            nc.gpsimd.affine_select(out=ident[:], in_=ident[:], compare_op=ALU.not_equal, fill=1.0,
                                    base=0, pattern=[[-1, P]], channel_multiplier=1)
            pool.drain().then_inc(const_done, 1)
            pool.dma_start(wrs[:], Wr).then_inc(w_in, 16)
            pool.dma_start(b2s[:], b2).then_inc(w_in, 16)
            pool.dma_start(gb[:, 0:1], gamma.rearrange("(d o) -> d o", o=1)).then_inc(w_in, 16)
            pool.dma_start(gb[:, 1:2], beta.rearrange("(d o) -> d o", o=1)).then_inc(w_in, 16)
            pool.dma_start(brb[:], row(br, E)).then_inc(w_in, 16)
            with nc.allow_non_contiguous_dma(reason="8 KiB of biases, once"):
                pool.dma_start(bcol[:], b1.rearrange("e (k h) -> h e k", h=P)).then_inc(w_in, 16)
            pool.wait_ge(pro_dve, 1)
            nc.gpsimd.partition_all_reduce(gmax[:, 1:2], gmax[:, 0:1], P,
                                           bass.bass_isa.ReduceOp.max).then_inc(pro_dve, 1)

            def rows2(s):
                pool.dma_start(xs[:], x_v[:, ds(s * SB, SB), :]).then_inc(x2_in, 16)
                pool.dma_start(h0s, h0_v[:, ds(s * SB, SB), :]).then_inc(x2_in, 16)
                pool.dma_start(ft, feat_v[:, ds(s * SB, SB), :]).then_inc(x2_in, 16)

            pool.wait_ge(v2_done, S)
            rows2(0)
            with pool.Fori(1, S, 1) as s:
                pool.wait_ge(v2_done, S)
                pool.wait_ge(x_used, s)
                rows2(s)

        @block.scalar
        def _(act):
            act.wait_ge(ln_done, 1)
            nc.scalar.activation(tmpa, xn, ACT.Square).then_inc(sq_done, 1)
            act.wait_ge(ln_done, 2)
            nc.scalar.activation(rstd[:], pf[:, 0], ACT.Sqrt).then_inc(sq_done, 1)
            act.wait_ge(a_in, 48)
            nc.scalar.activation(coe[:, 5:10], coe[:, 0:5], ACT.Exp, scale=-1.0).then_inc(pro_act, 1)
            act.wait_ge(pro_dve, 3)
            nc.scalar.activation(pf[:, 8:12], pf[:, 4:8], ACT.Exp).then_inc(pro_act, 1)
            act.wait_ge(pro_pe, 1)
            nc.scalar.activation(thrT, bank[7][0:T, 0:P], ACT.Copy).then_inc(pro_act, 2)
            act.wait_ge(pro_dve, 4)

            def edge_signs(c, landed):
                act.wait_ge(adj_in[c], landed)
                nc.scalar.activation(natb[:, c], adjc[:, c], ACT.Sign).then_inc(gt_done, 1)

            def positive_masks(s, jt, pair, p, coded=False):
                for q in range(2):
                    if not coded:
                        act.wait_ge(code_done, pair * 2 + (q + 1))
                    act.wait_ge(ring_free, pair * 2 + (q + 1))
                    nc.scalar.activation(ring[:, 0, (2 * p + q) % 4, :],
                                               edges[:, ds((jt + q) * N + s * W, W)], ACT.Relu,
                                               bias=kpow[:, 1, ds(jt + q, 1)], scale=kpow[:, 0, ds(jt + q, 1)]
                                         ).then_inc(pos_ready, 1)

            def evacuate(s, pairs, weights):
                act.wait_ge(ring_free, pairs * 2 + RING)
                for t in range(SB):
                    nc.scalar.activation(t1[:, t, :], acc[t][:, 0:2 * F], ACT.Copy,
                                         scale=weights(s, t)).then_inc(evac_done, 1)

            def row_weight(s, t):
                return wts[:, ds(s * SB + t, 1), 0]

            def row_scale(s, t):
                return cc[:, ds(s * SB + t, 1), 0]

            def normal_rows(s):
                act.wait_ge(rows_ready, s + 1)
                for t in range(SB):
                    ins = nc.scalar.activation(xs[:, t, :], xs[:, t, :], ACT.Identity,
                                               scale=loc[:, 14, t:t + 1], bias=loc[:, 15, t:t + 1])
                ins.then_inc(xn_ready, 1)

            def step(s, b, prev=None, last=False):
                n = s * B + b
                edge_signs(1, n * 16 + 16)
                for p in range(BP):
                    if p == BP // 2 and not last:
                        edge_signs(0, n * 16 + 32)
                    positive_masks(s, b * JB + 2 * p, n * BP + p, p)
                    if prev is not None and p == 1:
                        evacuate(prev, s * PAIRS, row_weight)
                if prev is not None:
                    normal_rows(prev)

            def superblock(s, first=False, last=False):
                step(s, 0, None if first else s - 1)
                for b in range(1, B):
                    step(s, b, last=last and b == B - 1)

            edge_signs(0, 16)
            superblock(0, first=True)
            with act.Fori(1, S - 1, 1) as s:
                superblock(s)
            superblock(S - 1, last=True)
            evacuate(S - 1, S * PAIRS, row_weight)
            normal_rows(S - 1)

            def gelu(s, e):
                for k in range(HH):
                    act.wait_ge(h_done, s * (E * HH) + (e * HH + k + 1))
                    if k == 0:
                        act.wait_ge(y_done, s * E + (e + 1))
                    nc.scalar.activation(hT[e % 2][:, k, :], hb[k][:], ACT.Gelu,
                                         bias=bcol[:, e, k:k + 1]).then_inc(h_ready, 1)

            def propagate(s, front, tail):
                for p in range(PAIRS):
                    if tail is not None and p < E - (FE - 1):
                        gelu(tail, FE - 1 + p)
                    if front is not None and p > PAIRS - FE:
                        gelu(front, p - (PAIRS - FE) - 1)
                    if s is not None:
                        positive_masks(s, 2 * p, (s + S) * PAIRS + p, p, coded=True)
                    if front is None:
                        continue
                    if p == 1:
                        evacuate(front, front * PAIRS + (S + 1) * PAIRS, row_scale)
                    if p == 5:
                        act.wait_ge(ln2_var, front + 1)
                        nc.scalar.activation(loc[:, 8, :], loc[:, 7, :], ACT.Sqrt).then_inc(ln2_sqrt, 1)
                    if p == 10:
                        act.wait_ge(gap_ready, front + 1)
                        nc.scalar.activation(small[:, 1, 0:SB], small[:, 0, 0:SB], ACT.Exp).then_inc(gap_exp, 1)

            propagate(0, None, None)
            propagate(1, 0, None)
            with act.Fori(2, S, 1) as s:
                propagate(s, s - 1, s - 2)
            propagate(None, S - 1, S - 2)
            propagate(None, None, S - 1)

        @block.vector
        def _(dve):
            def bc(ap, n=T):
                return ap.unsqueeze(2).to_broadcast([P, n, F])

            dve.wait_ge(x_in, 16)
            nc.vector.tensor_reduce(mean[:], xn, X, ALU.add)
            dve.drain()
            nc.vector.tensor_scalar(mean[:], mean[:], 1.0 / F, None, ALU.mult)
            dve.drain()
            nc.vector.tensor_tensor(xn, xn, bc(mean[:]), ALU.subtract).then_inc(ln_done, 1)
            dve.wait_ge(sq_done, 1)
            nc.vector.tensor_reduce(pf[:, 0], tmpa, X, ALU.add)
            dve.drain()
            nc.vector.tensor_scalar(pf[:, 0], pf[:, 0], 1.0 / F, EPS, ALU.mult, ALU.add).then_inc(ln_done, 1)
            dve.wait_ge(sq_done, 2)
            nc.vector.reciprocal(rstd[:], rstd[:])
            dve.drain()
            nc.vector.tensor_tensor(xn, xn, bc(rstd[:]), ALU.mult)
            dve.wait_ge(a_in, 48)
            dve.drain()
            nc.vector.tensor_tensor(tmpa, xn, ab[:, 0, :].unsqueeze(1).to_broadcast([P, T, F]), ALU.mult)
            nc.vector.tensor_tensor(tmpb, xn, ab[:, 1, :].unsqueeze(1).to_broadcast([P, T, F]), ALU.mult)
            dve.drain().then_inc(ln_done, 1)
            nc.vector.tensor_reduce(pf[:, 1], tmpa, X, ALU.add)
            nc.vector.tensor_reduce(pf[:, 2], tmpb, X, ALU.add)
            dve.drain()
            nc.vector.tensor_scalar(pf[:, 3], pf[:, 1], -1.0, None, ALU.mult).then_inc(ln_done, 1)
            nc.vector.tensor_reduce(gmax[:, 0:1], pf[:, 2], X, ALU.max).then_inc(pro_dve, 1)
            dve.wait_ge(pro_act, 1)
            nc.vector.tensor_scalar(coe[:, 5:10], coe[:, 5:10], 1.0, None, ALU.add)
            dve.drain()
            nc.vector.reciprocal(coe[:, 0:5], coe[:, 5:10])
            dve.drain()
            nc.vector.tensor_scalar(coe[:, 5:10], coe[:, 0:5], -1.0, 1.0, ALU.mult, ALU.add)
            dve.drain()
            nc.vector.tensor_tensor(coe[:, 10:11], coe[:, 6:7], coe[:, 0:1], ALU.mult)
            nc.vector.tensor_tensor(coe[:, 11:12], coe[:, 6:7], coe[:, 5:6], ALU.mult)
            nc.vector.tensor_scalar(coe[:, 8:9], coe[:, 3:4], -1.0, None, ALU.mult)
            dve.wait_ge(pro_dve, 2)
            nc.vector.tensor_scalar(pf[:, 4], pf[:, 2], gmax[:, 1:2], None, ALU.subtract)
            nc.vector.tensor_scalar(pf[:, 6], pf[:, 1], gmax[:, 1:2], None, ALU.add)
            dve.drain()
            nc.vector.tensor_scalar(pf[:, 5], pf[:, 4], 0.2, HEADROOM, ALU.mult, ALU.add)
            nc.vector.tensor_scalar(pf[:, 7], pf[:, 6], 0.2, None, ALU.mult)
            dve.drain()
            nc.vector.tensor_scalar(pf[:, 4], pf[:, 4], HEADROOM, None, ALU.add)
            nc.vector.tensor_tensor(pf[:, 12], pf[:, 6], pf[:, 7], ALU.max)
            dve.drain()
            nc.vector.tensor_tensor(pf[:, 6], pf[:, 6], pf[:, 12], ALU.subtract)
            nc.vector.tensor_tensor(pf[:, 7], pf[:, 7], pf[:, 12], ALU.subtract)
            dve.drain().then_inc(pro_dve, 1)
            dve.wait_ge(pro_act, 2)
            fac = pf[:, 8:10].bitcast(U32)
            nc.vector.tensor_scalar(pf[:, 13:15].bitcast(U32), fac, 0x7F800000, None, ALU.bitwise_and)
            nc.vector.tensor_scalar(pf[:, 15:17].bitcast(U32), fac, 0x007FFFFF, 0x3F800000,
                                    ALU.bitwise_and, ALU.bitwise_or)
            dve.drain()
            nc.vector.tensor_copy(kpow[:, 0], pf[:, 13])
            nc.vector.tensor_scalar(kpow[:, 1], pf[:, 13], -2.0, None, ALU.mult)
            nc.vector.tensor_copy(kpow[:, 2], pf[:, 14])
            nc.vector.tensor_scalar(mant[:], pf[:, 15:17], VS, None, ALU.mult)
            sqv = sq[:].rearrange("p t g (k c) -> p g t k c", k=2)
            nc.vector.tensor_tensor(pf[:, 17:19], pf[:, 15:17], pf[:, 15:17], ALU.mult)
            nc.vector.tensor_scalar(pf[:, 19:21], pf[:, 13:15], QS, None, ALU.mult)
            dve.drain()
            nc.vector.tensor_tensor(pf[:, 17:19], pf[:, 17:19], pf[:, 19:21], ALU.mult)
            dve.drain()
            for k, src in enumerate((pf[:, 15:17], pf[:, 17:19])):
                for c in range(3):
                    nc.vector.tensor_copy(sqv[:, :, :, k, c], src)
                    dve.drain()
                    if c < 2:
                        nc.vector.tensor_tensor(src, src, sqv[:, :, :, k, c], ALU.subtract)
                        dve.drain()
            nc.vector.tensor_copy(wts[:, :, 0], pf[:, 10])
            nc.vector.tensor_copy(wts[:, :, 2], pf[:, 11])
            nc.vector.tensor_tensor(wts[:, :, 1], pf[:, 10], pf[:, 10], ALU.mult)
            nc.vector.tensor_tensor(wts[:, :, 3], pf[:, 11], pf[:, 11], ALU.mult)
            dve.wait_ge(pro_pe, 2)
            nc.vector.tensor_copy(colmean[:], bank[6][:, 0:F])

            def split(src, g, t0, n, scratch):
                nc.vector.tensor_tensor(scratch, src, bc(mant[:, g, t0:t0 + n], n), ALU.mult)
                dve.drain()
                nc.vector.tensor_copy(v[:, g, t0:t0 + n, 0:F], scratch)
                dve.drain()
                return nc.vector.tensor_tensor(v[:, g, t0:t0 + n, F:2 * F], scratch,
                                               v[:, g, t0:t0 + n, 0:F], ALU.subtract)

            nc.vector.tensor_copy(f2[:], pf[:, 2])
            split(xn, 0, 0, T, tmpa)
            split(xn, 1, 0, T, tmpb)
            dve.drain().then_inc(v_done, 1)
            dve.drain().then_inc(pro_dve, 1)

            def codes(s, b, n, p):
                dve.wait_ge(tp_done, n * BP + (p + 1))
                for q in (2 * p, 2 * p + 1):
                    jt = b * JB + q
                    nc.vector.scalar_tensor_tensor(
                        edges[:, ds(jt * N + s * W, W)], thr[:, 1, :], f2[:, ds(jt, 1)],
                        tp[p % 2][:].bitcast(F16)[:, (q % 2) * W:(q % 2 + 1) * W], ALU.is_lt, ALU.add
                    ).then_inc(code_done, 1)

            def negative_masks(s, jt, pair, p, coded=False):
                for q in range(2):
                    dve.wait_ge(ring_free, pair * 2 + (q + 1))
                    if not coded:
                        dve.wait_ge(code_done, pair * 2 + (q + 1))
                    nc.vector.tensor_scalar(ring[:, 1, (2 * p + q) % 4, :],
                                                  edges[:, ds((jt + q) * N + s * W, W)], 2.0,
                                                  kpow[:, 2, ds(jt + q, 1)], ALU.is_equal, ALU.mult
                                            ).then_inc(neg_ready, 1)

            def combine(s, evacuated, weights):
                for t in range(SB):
                    dve.wait_ge(evac_done, evacuated + (t + 1))
                    nc.vector.scalar_tensor_tensor(t1[:, t, :], acc[t][:, 2 * F:4 * F], weights(s, t),
                                                   t1[:, t, :], ALU.mult, ALU.add).then_inc(acc_free, 1)
                dve.drain()

            raw = loc[:, 2:6].rearrange("p k t -> p (k t)")
            factors = raw.rearrange("p (t g) -> p t g", g=4)

            def read_squares(pairs):
                dve.wait_ge(ring_free, pairs * 2 + RING)
                nc.vector.tensor_reduce(raw, sqb[:, 0:SB * 12].rearrange("p (g c) -> p g c", c=3), X, ALU.add)
                dve.drain()

            def softmax_sums(s):
                sl = ds(s * SB, SB)
                nc.vector.tensor_tensor(factors, factors, wts[:, sl, :], ALU.mult)
                dve.drain()
                nc.vector.tensor_tensor(factors[:, :, 0:2], factors[:, :, 0:2], factors[:, :, 2:4], ALU.add)
                dve.drain()
                nc.vector.tensor_scalar(loc[:, 6], factors[:, :, 0], 0.0, None, ALU.is_equal)
                dve.drain()
                nc.vector.tensor_tensor(loc[:, 7], factors[:, :, 0], loc[:, 6], ALU.add)
                dve.drain()
                nc.vector.reciprocal(loc[:, 8], loc[:, 7])
                dve.drain()
                nc.vector.tensor_scalar(loc[:, 9], loc[:, 8], 1.0 / VS, None, ALU.mult)
                nc.vector.tensor_tensor(loc[:, 10], factors[:, :, 1], loc[:, 8], ALU.mult)
                dve.drain()

            def row_scales(s):
                sl = ds(s * SB, SB)
                nc.vector.tensor_tensor(cc[:, sl, 0], loc[:, 9], wts[:, sl, 0], ALU.mult)
                nc.vector.tensor_tensor(cc[:, sl, 1], loc[:, 9], wts[:, sl, 2], ALU.mult)
                nc.vector.tensor_copy(cc[:, sl, 2], loc[:, 6])
                nc.vector.scalar_tensor_tensor(loc[:, 11], loc[:, 10], 0.5 / QS, loc[:, 8], ALU.mult, ALU.mult)
                dve.drain()
                nc.vector.scalar_tensor_tensor(rs[:, sl], loc[:, 6], 0.5 / N, loc[:, 11], ALU.mult, ALU.add)
                dve.drain()
                nc.vector.tensor_scalar(loc[:, 13], rs[:, sl], -1.0, coe[:, 7:8], ALU.mult, ALU.add)
                dve.drain()
                nc.vector.tensor_tensor(loc[:, 14], loc[:, 13], rstd[:, sl], ALU.mult)
                dve.drain()
                nc.vector.scalar_tensor_tensor(loc[:, 15], mean[:, sl], -1.0, loc[:, 14], ALU.mult, ALU.mult)
                dve.wait_ge(xs_in, s * 16 + 16)
                nc.vector.tensor_copy(loc[:, 12], loc[:, 9])
                dve.drain().then_inc(rows_ready, 1)

            def features(s):
                dve.wait_ge(xn_ready, s + 1)
                for half in (t1[:, :, 0:F], t1[:, :, F:2 * F]):
                    for t in range(SB):
                        nc.vector.scalar_tensor_tensor(xs[:, t, :], half[:, t, :], loc[:, 12, t:t + 1],
                                                       xs[:, t, :], ALU.mult, ALU.add)
                    dve.drain()
                for t in range(SB):
                    nc.vector.scalar_tensor_tensor(xs[:, t, :], colmean[:], loc[:, 6, t:t + 1],
                                                   xs[:, t, :], ALU.mult, ALU.add)
                dve.drain()
                nc.vector.tensor_scalar(t1[:, :, 0:F], xs[:], -THRESH, THRESH, ALU.max, ALU.min)
                dve.drain()
                nc.vector.tensor_tensor(xs[:], xs[:], t1[:, :, 0:F], ALU.subtract).then_inc(feat_ready, 1)

            def row_weight(s, t):
                return wts[:, ds(s * SB + t, 1), 2]

            def row_scale(s, t):
                return cc[:, ds(s * SB + t, 1), 1]

            def step(s, b, prev=None):
                n = s * B + b
                for p in range(BP):
                    codes(s, b, n, p)
                    if p:
                        negative_masks(s, b * JB + 2 * (p - 1), n * BP + (p - 1), p - 1)
                    if prev is not None:
                        if p == 1:
                            read_squares(s * PAIRS)
                            combine(prev, prev * SB, row_weight)
                        if p == 2:
                            softmax_sums(prev)
                            row_scales(prev)
                negative_masks(s, b * JB + 2 * (BP - 1), n * BP + (BP - 1), BP - 1)
                if prev is not None:
                    features(prev)

            def superblock(s, first=False):
                dve.wait_ge(thr_in, s * 16 + 16)
                nc.vector.tensor_copy(thr[:, 1, :], thr[:, 0, :])
                dve.drain().then_inc(thr_free, 1)
                step(s, 0, None if first else s - 1)
                with dve.Fori(1, B, 1) as b:
                    step(s, b)

            superblock(0, first=True)
            with dve.Fori(1, S, 1) as s:
                superblock(s)
            read_squares(S * PAIRS)
            combine(S - 1, (S - 1) * SB, row_weight)
            softmax_sums(S - 1)
            row_scales(S - 1)
            features(S - 1)

            dve.wait_ge(f_in, 16)
            for g in range(S):
                src = feats[:, g * SB:(g + 1) * SB]
                pr = prod.rearrange("p (t d) -> p t d", d=F)
                split(src, 0, g * SB, SB, pr)
                dve.drain()
                split(src, 1, g * SB, SB, pr)
                dve.drain().then_inc(v2_done, 1)
            dve.wait_ge(mean_done, 1)
            nc.vector.tensor_copy(colmean[:], bank[7][:, 0:F])
            dve.wait_ge(w_in, 96)

            def attended(s):
                sl = ds(s * SB, SB)
                nc.vector.tensor_copy(loc[:, 6], cc[:, sl, 2])
                nc.vector.tensor_scalar(loc[:, 2], rs[:, sl], coe[:, 1:2], coe[:, 10:11], ALU.mult, ALU.add)
                nc.vector.tensor_tensor(t1[:, :, 0:F], t1[:, :, 0:F], t1[:, :, F:2 * F], ALU.add)
                dve.drain()
                for t in range(SB):
                    nc.vector.scalar_tensor_tensor(t1[:, t, 0:F], colmean[:], loc[:, 6, t:t + 1],
                                                   t1[:, t, 0:F], ALU.mult, ALU.add)
                dve.drain()
                dve.wait_ge(x2_in, s * 48 + 48)

            def layer_rows(s):
                pu = t1[:, :, 0:F]
                nc.vector.scalar_tensor_tensor(ft, pu, coe[:, 8:9], ft, ALU.mult, ALU.add)
                nc.vector.scalar_tensor_tensor(xs[:], pu, coe[:, 1:2], xs[:], ALU.mult, ALU.add)
                dve.drain()
                nc.vector.scalar_tensor_tensor(xs[:], h0s, coe[:, 11:12], xs[:], ALU.mult, ALU.add)
                dve.drain()
                for t in range(SB):
                    nc.vector.scalar_tensor_tensor(xs[:, t, :], ft[:, t, :], loc[:, 2, t:t + 1], xs[:, t, :],
                                                   ALU.mult, ALU.add)
                dve.drain()

            def norm_stats():
                for t in range(SB):
                    nc.vector.bn_stats(small[:, 2 + t, 0:6], xs[:, t, :])
                dve.drain()
                for t in range(SB):
                    nc.vector.bn_aggr(loc[:, 9:11, t], small[:, 2 + t, 0:6])
                dve.drain()
                nc.vector.tensor_scalar(loc[:, 11], loc[:, 10], EPS, EPS, ALU.add, ALU.mult)
                dve.drain()
                nc.vector.tensor_tensor(loc[:, 7], loc[:, 11], loc[:, 10], ALU.add).then_inc(ln2_var, 1)

            def norm_rows(s):
                dve.wait_ge(ln2_sqrt, s + 1)
                nc.vector.reciprocal(loc[:, 12], loc[:, 8])
                dve.drain()
                for t in range(SB):
                    ins = nc.vector.tensor_scalar(t1[:, t, 0:F], xs[:, t, :], loc[:, 9, t:t + 1],
                                                  loc[:, 12, t:t + 1], ALU.subtract, ALU.mult)
                ins.then_inc(xn2_ready, 1)

            def norm_columns(s):
                dve.wait_ge(xT_done, s + 1)
                nc.vector.tensor_scalar(xnT, hb[0][:], gb[:, 0:1], gb[:, 1:2], ALU.mult, ALU.add).then_inc(xT_ready, 1)

            def two_largest(s):
                dve.wait_ge(lg_done, s + 1)
                nc.vector.tensor_tensor(lg[:], hb[1][:, 0:SB * E].rearrange("p (t e) -> p t e", e=E),
                                        brb[:].unsqueeze(1).to_broadcast([P, SB, E]), ALU.add)
                dve.drain()
                for t in range(SB):
                    nc.vector.max(top[:, t, :], lg[:, t, :])
                dve.drain()
                for t in range(SB):
                    nc.vector.max_index(tix[:, t, :], top[:, t, :], lg[:, t, :])
                nc.vector.tensor_tensor(small[:, 0, 0:SB], top[:, :, 1], top[:, :, 0], ALU.subtract).then_inc(gap_ready, 1)
                dve.drain()
                nc.vector.tensor_copy(top[:, :, 2:4], tix[:, :, 0:2])

            def expert_weights(s):
                dve.wait_ge(gap_exp, s + 1)
                nc.vector.tensor_scalar(loc[:, 13], small[:, 1, 0:SB], 1.0, None, ALU.add)
                dve.drain()
                nc.vector.reciprocal(loc[:, 14], loc[:, 13])
                dve.drain()
                nc.vector.tensor_tensor(loc[:, 15], loc[:, 14], small[:, 1, 0:SB], ALU.mult)
                dve.drain()
                for t in range(SB):
                    for k in range(2):
                        nc.vector.tensor_scalar(wf[:, k, t, :], iota[:], top[:, t, 2 + k:3 + k],
                                                loc[:, 14 + k, t:t + 1], ALU.is_equal, ALU.mult)
                dve.drain()
                nc.vector.tensor_tensor(wf[:, 0], wf[:, 0], wf[:, 1], ALU.add).then_inc(wf_ready, 1)

            def expert_biases(s):
                dve.wait_ge(wT_done, s + 1)
                nc.vector.tensor_copy(wT, yb[1][0:E, :]).then_inc(wT_ready, 1)
                dve.wait_ge(b2_done, s + 1)
                dve.wait_ge(x2_free, s + 1)
                nc.vector.tensor_tensor(x2[:], xs[:], yb[0][:].rearrange("p (t d) -> p t d", d=F), ALU.add).then_inc(b2_added, 1)
                dve.drain().then_inc(x_used, 1)

            def add_expert(s, e):
                dve.wait_ge(y_done, s * E + (e + 3))
                if e == 0:
                    dve.wait_ge(b2_added, s + 1)
                else:
                    dve.wait_ge(y_added, s * E + (e + 1))
                for t in range(SB):
                    ins = nc.vector.scalar_tensor_tensor(
                        x2[:, t, :], yb[(e + 1) % 2][:, t * F:(t + 1) * F], wf[:, 0, t, e:e + 1],
                        x2[:, t, :], ALU.mult, ALU.add)
                ins.then_inc(y_added, 1)

            def propagate(s, front, tail):
                for p in range(PAIRS):
                    if s is not None:
                        negative_masks(s, 2 * p, (s + S) * PAIRS + p, p, coded=True)
                    if tail is not None and p < E - (FE - 2):
                        add_expert(tail, FE - 2 + p)
                        if FE - 2 + p == E - 1:
                            dve.drain().then_inc(out_ready, 1)
                    if front is None:
                        continue
                    if p == 1:
                        combine(front, (front + S) * SB, row_scale)
                    if p == 2:
                        attended(front)
                    if p == 3:
                        layer_rows(front)
                    if p == 4:
                        norm_stats()
                    if p == 5:
                        norm_rows(front)
                    if p == 7:
                        norm_columns(front)
                    if p == 9:
                        two_largest(front)
                    if p == 10:
                        expert_weights(front)
                    if p == 12:
                        expert_biases(front)
                    if p > PAIRS - FE + 1:
                        add_expert(front, p - (PAIRS - FE + 2))

            propagate(0, None, None)
            propagate(1, 0, None)
            with dve.Fori(2, S, 1) as s:
                propagate(s, s - 1, s - 2)
            propagate(None, S - 1, S - 2)
            propagate(None, None, S - 1)

        @block.tensor
        def _(pe):
            pe.sem_inc(ring_free, RING)
            pe.sem_inc(acc_free, SB)
            pe.wait_ge(const_done, 1)
            pe.wait_ge(ln_done, 4)
            nc.tensor.transpose(bank[7][0:T, 0:P], pf[:, 3], ident[:]).then_inc(pro_pe, 1)
            for t in range(T):
                mm = nc.tensor.matmul(bank[6][:, 0:F], meancol[:].to_broadcast([P, P]), xn[:, t, :], start=(t == 0), stop=(t == T - 1))
            mm.then_inc(pro_pe, 1)
            pe.wait_ge(v_done, 1)

            def turn(p, chunks):
                pe.wait_ge(gt_done, chunks)
                for q in range(2):
                    for t in range(SB):
                        k = (2 * p + q) % CH
                        tr = nc.tensor.transpose(
                            tp[p % 2][:].bitcast(BF16)[:, q * W + t * P:q * W + (t + 1) * P],
                            natb[:, (p * 2) // CH % 2, t, k * P:(k + 1) * P], identb[:])
                tr.then_inc(tp_done, 1)

            def sums(s, jt, pair, p, first, squares, before=0):
                for q in range(2):
                    pe.wait_ge(pos_ready, pair * 2 + (q + 1))
                    pe.wait_ge(neg_ready, pair * 2 + (q + 1))
                    lead = first and q == 0
                    for t in range(SB):
                        if lead:
                            pe.wait_ge(acc_free, s * SB + (before * SB + t + 1))
                        for g in range(2):
                            lhs = ring[:, g, (2 * p + q) % 4, t * P:(t + 1) * P]
                            mm = nc.tensor.matmul(acc[t][:, g * 2 * F:(g + 1) * 2 * F], lhs, v[:, g, ds(jt + q, 1), :],
                                                  start=lead and g == 0, stop=False, skip_group_check=True)
                            if squares:
                                o = (t * 2 + g) * 6
                                mm = nc.tensor.matmul(sqb[:, o:o + 6], lhs, sq[:, ds(jt + q, 1), g, :],
                                                      start=lead and g == 0 and t == 0, stop=False,
                                                      skip_group_check=True)
                    mm.then_inc(ring_free, 1)

            def step(s, b, first=False, last=False):
                n = s * B + b
                for p in range(BP):
                    if p < BP - 2 or not last:
                        pe.wait_ge(code_done, (n * BP + p) * 2 + 2)
                        turn((p + 2) % BP, n * 2 + ((p + 2) // 2 + 1))
                    sums(s, b * JB + 2 * p, n * BP + p, p, first and p == 0, True)

            def superblock(s, last=False):
                step(s, 0, first=True)
                with pe.Fori(1, B - 1 if last else B, 1) as b:
                    step(s, b)
                if last:
                    step(s, B - 1, last=True)

            turn(0, 1)
            turn(1, 1)
            with pe.Fori(0, S - 1, 1) as s:
                superblock(s)
            superblock(S - 1, last=True)

            pe.wait_ge(f_in, 16)
            for t in range(T):
                mm = nc.tensor.matmul(bank[7][:, 0:F], meancol[:].to_broadcast([P, P]), feats[:, t, :], start=(t == 0), stop=(t == T - 1))
            mm.then_inc(mean_done, 1)
            pe.sem_inc(y_done, 2)
            pe.sem_inc(y_added, 1)

            def rows_to_columns(s):
                pe.wait_ge(xn2_ready, s + 1)
                for t in range(SB):
                    tr = nc.tensor.transpose(hb[0][:, t * P:(t + 1) * P], t1[:, t, 0:F], ident[:])
                tr.then_inc(xT_done, 1)

            def logits(s):
                pe.wait_ge(xT_ready, s + 1)
                for t in range(SB):
                    mm = nc.tensor.matmul(hb[1][:, t * E:(t + 1) * E], xnT[:, t * P:(t + 1) * P], wrs[:],
                                          start=True, stop=True)
                mm.then_inc(lg_done, 1)

            def weights_to_columns(s):
                pe.wait_ge(wf_ready, s + 1)
                pe.wait_ge(y_added, s * E + 1)
                for t in range(SB):
                    tr = nc.tensor.transpose(yb[1][0:E, t * P:(t + 1) * P], wf[:, 0, t, :], ident[:])
                tr.then_inc(wT_done, 1)

            def expert_biases(s):
                pe.wait_ge(wT_ready, s + 1)
                for t in range(SB):
                    mm = nc.tensor.matmul(yb[0][:, t * F:(t + 1) * F], wT[:, t * P:(t + 1) * P], b2s[:],
                                          start=True, stop=True)
                mm.then_inc(b2_done, 1)

            def hidden(s, e):
                for k in range(HH):
                    if e == 0 and k:
                        pe.wait_ge(gap_ready, s + 1)
                    if e:
                        pe.wait_ge(h_ready, s * (E * HH) + (e * HH + k - 1))
                    nc.tensor.matmul(hb[k][:], w1s[:, e, k * P:(k + 1) * P], xnT,
                                     start=True, stop=True).then_inc(h_done, 1)

            def expert_rows(s, e):
                pe.wait_ge(h_ready, s * (E * HH) + (e * HH + 2))
                pe.wait_ge(y_added, s * E + max(e, 1))
                if e == 1:
                    pe.wait_ge(b2_added, s + 1)
                for t in range(SB):
                    for k in range(HH):
                        mm = nc.tensor.matmul(yb[(e + 1) % 2][:, t * F:(t + 1) * F],
                                              hT[e % 2][:, k, t * P:(t + 1) * P], w2s[:, e, k, :],
                                              start=(k == 0), stop=(k == HH - 1))
                mm.then_inc(y_done, 1)

            def propagate(s, front, tail):
                for p in range(PAIRS):
                    if s is not None:
                        if front is None and p % 2 == 0:
                            pe.wait_ge(v2_done, p // 2 + 1)
                        sums(s, 2 * p, (s + S) * PAIRS + p, p, p == 0, False, S)
                    if tail is not None and p < E - FE:
                        if FE + p + 1 < E:
                            hidden(tail, FE + p + 1)
                        expert_rows(tail, FE + p)
                    if front is None:
                        continue
                    if p == 5:
                        rows_to_columns(front)
                    if p == 7:
                        logits(front)
                    if p == 9:
                        hidden(front, 0)
                    if p == 10:
                        weights_to_columns(front)
                    if p == 11:
                        expert_biases(front)
                    if p >= PAIRS - FE:
                        hidden(front, p - (PAIRS - FE) + 1)
                        expert_rows(front, p - (PAIRS - FE))

            pe.wait_ge(w_in, 96)
            propagate(0, None, None)
            pe.wait_ge(weights_in, 32)
            propagate(1, 0, None)
            with pe.Fori(2, S, 1) as s:
                propagate(s, s - 1, s - 2)
            propagate(None, S - 1, S - 2)
            propagate(None, None, S - 1)


_INS = ["x", "adj", "L0_gnn_h0", "L0_gnn_a", "L0_gnn_temp", "L0_ffn_gamma", "L0_ffn_beta", "L0_ffn_Wr",
        "L0_ffn_br", "L0_ffn_W1", "L0_ffn_b1", "L0_ffn_W2", "L0_ffn_b2"]


def kernel(**inputs):
    import numpy as _np
    import concourse.bacc as _bacc
    from concourse import mybir as _mybir
    from concourse.bass_utils import run_bass_kernel_spmd as _run

    nc = _bacc.Bacc("TRN2", target_bir_lowering=False, num_devices=1, dynamic_dma_scratch_size=8192)
    arrays, args = {}, []
    for name in _INS:
        arr = _np.ascontiguousarray(inputs[name])
        arrays[f"in_{name}"] = arr
        args.append(nc.dram_tensor(f"in_{name}", arr.shape, _mybir.dt.from_np(arr.dtype), kind="ExternalInput").ap())
    args.append(nc.dram_tensor("out_x", (N, F), F32, kind="ExternalOutput").ap())
    program(nc, *args)
    r = _run(nc, [arrays], core_ids=[0])
    return r.results[0]["out_x"]
```

```python
from contextlib import ExitStack

import concourse.bass as bass
from concourse import mybir

P = 128
N = 4096
F = 128
T = N // P
SB = 4
W = SB * P
S = T // SB
CH = 4
JB = 2 * CH
B = T // JB
E = 8
H = 256
HH = H // P
EPS = 1e-5
THRESH = 1e-6
HEADROOM = 60.0
VS = 512.0
QS = 2.0 ** -60

F32 = mybir.dt.float32
BF16 = mybir.dt.bfloat16
F16 = mybir.dt.float16
U8 = mybir.dt.uint8
U32 = mybir.dt.uint32
ALU = mybir.AluOpType
ACT = mybir.ActivationFunctionType
X = mybir.AxisListType.X


def program(nc, x, adj, h0, a, temp, gamma, beta, Wr, br, W1, b1, W2, b2, out):
    with ExitStack() as ctx:
        def sb(name, shape, dt=F32):
            return ctx.enter_context(nc.sbuf_tensor(name, shape, dt))

        def sem(name):
            return ctx.enter_context(nc.semaphore(name))

        ds = bass.ds
        XG = 4
        NG = T // SB
        feat_dram = nc.dram_tensor("feat_dram", (N, F), F32, kind="Internal").ap()
        thr_dram = nc.dram_tensor("thr_dram", (T, P), F32, kind="Internal").ap()

        edges = sb("edges", [P, T * N], U8)
        stage = sb("stage", [P, 4096])
        nat = sb("nat", [P, 2048])
        thr = sb("thr", [P, 2, W])
        v = sb("v", [P, 2, T, 2 * F], F16)
        sq = sb("sq", [P, T, 2, 6], BF16)
        ring = sb("ring", [P, 2, 4, W], BF16)
        t1 = sb("t1", [P, SB, 2 * F])
        xs = sb("xs", [P, SB, F])
        colmean = sb("colmean", [P, F])
        identb = sb("identb", [P, P], BF16)
        ident = sb("ident", [P, P])
        mean = sb("mean", [P, T])
        rstd = sb("rstd", [P, T])
        kpow = sb("kpow", [P, 3, T])
        mant = sb("mant", [P, 2, T])
        wts = sb("wts", [P, T, 4])
        cc = sb("cc", [P, T, 3])
        rs = sb("rs", [P, T])
        coe = sb("coe", [P, 12])
        f2 = sb("f2", [P, T])
        meancol = sb("meancol", [P, 1])
        loc = sb("loc", [P, 16, SB])
        small = sb("small", [P, 6, 8])
        acol = sb("acol", [P, 2])
        xn = edges[:, 28 * N:32 * N].bitcast(F32).rearrange("p (t d) -> p t d", d=F)
        xnt = edges[:, 24 * N:28 * N].bitcast(F32)
        pro = edges[:, 20 * N:24 * N].bitcast(F32)
        pf = pro[:, 0:1024].rearrange("p (k t) -> p k t", t=T)
        gmax = pro[:, 1024:1026]
        nbias = pro[:, 1056:1088]
        thrT = pro[0:T, 1152:1280]
        stats = pro[:, 1280:1472].rearrange("p (t c) -> p t c", c=6)
        diag = pro[:, 1792:1920]
        colsum = pro[:, 1600:1601]
        quarter = pro[:, 1664:1792]
        meanvar = pro[:, 1536:1600].rearrange("p (t c) -> p t c", c=2)
        adjc = stage[:].rearrange("p (c t w) -> p c t w", c=2, t=SB)
        natb = nat[:].bitcast(BF16).rearrange("p (c t w) -> p c t w", c=2, t=SB)
        feats = stage[:].rearrange("p (t d) -> p t d", d=F)
        w1 = stage[:, 0:2048].bitcast(F16).rearrange("p (k e h) -> p k e h", k=2, e=E)
        w2s = stage[:, 2048:4096].rearrange("p (e k d) -> p e k d", e=E, k=HH)
        hT = [nat[:, 0:1024].rearrange("p (k w) -> p k w", k=HH),
              sb("hT1", [P, HH, W])]
        w1s = [part.rearrange("p k (e h) -> p (k e) h", h=H) for part in hT]
        z = sb("z", [P, 2, W], F16)
        bound = sb("bound", [P, 8])
        x2 = sb("x2", [P, SB, F])
        ft = nat[:, 1024:1536].rearrange("p (t d) -> p t d", d=F)
        h0s = nat[:, 1536:2048].rearrange("p (t d) -> p t d", d=F)
        xnT = thr[:, 0, :]
        wrs = sb("wrs", [P, E])
        b2s = sb("b2s", [E, F])
        bcol = sb("bcol", [P, E, HH])
        gb = sb("gb", [P, 2])
        brb = sb("brb", [P, E])
        iota = sb("iota", [P, E])
        lg = sb("lg", [P, SB, E])
        top = sb("top", [P, SB, 8])
        tix = sb("tix", [P, SB, 8], U32)
        wf = identb[:].bitcast(F32).rearrange("p (k t e) -> p k t e", k=2, t=SB)
        wT = thr[0:E, 1, :]

        bank = [ctx.enter_context(nc.psum_tensor(f"bank{i}", [P, 512], F32)) for i in range(8)]
        acc, sqb = bank[0:4], bank[4]
        tp = [bank[5], bank[6]]
        hb = [bank[5], bank[6]]
        yb = [bank[4], bank[7]]

        x_in = [sem(f"x_in{g}") for g in range(XG)]
        a_in, w_in = sem("a_in"), sem("w_in")
        const_done = sem("const_done")
        adj_in = [sem("adj_in0"), sem("adj_in1")]
        ln_done, sq_done = sem("ln_done"), sem("sq_done")
        norm_done = [sem("norm_dve"), sem("norm_act")]
        turned, copied = sem("turned"), [sem("copied_dve"), sem("copied_act")]
        hi_done = sem("hi_done")
        temp_in, temp_exp, f_done, f1_ready = sem("temp_in"), sem("temp_exp"), sem("f_done"), sem("f1_ready")
        f1_turned, f1_copied = sem("f1_turned"), sem("f1_copied")
        max_ready, max_done, exponents_ready = sem("max_ready"), sem("max_done"), sem("exponents_ready")
        factors_ready, parts_ready, squares_ready = sem("factors_ready"), sem("parts_ready"), sem("squares_ready")
        diag_ready, colmean_done, quarter_done = sem("diag_ready"), sem("colmean_done"), sem("quarter_done")
        thr_out, thr_in, thr_free = sem("thr_out"), sem("thr_in"), sem("thr_free")
        v_done = sem("v_done")
        gt_done, gt2_done, tp_done, code_done = sem("gt_done"), sem("gt2_done"), sem("tp_done"), sem("code_done")
        pos_ready, neg_ready, ring_free = sem("pos_ready"), sem("neg_ready"), sem("ring_free")
        evac_done, acc_free = sem("evac_done"), sem("acc_free")
        xs_in, feat_ready, feat_out = sem("xs_in"), sem("feat_ready"), sem("feat_out")
        sums_ready, inverse_ready = sem("sums_ready"), sem("inverse_ready")
        combined, rows_done = sem("combined"), sem("rows_done")
        f_in = [sem(f"f_in{k}") for k in range(3)]
        v2_done, weights_in = sem("v2_done"), sem("weights_in")
        w1_in, bounds_done, w1_split, z_ready = sem("w1_in"), sem("bounds_done"), sem("w1_split"), sem("z_ready")
        mean_done = sem("mean_done")
        x2_in, ln2_var, ln2_sqrt, xn2_ready = sem("x2_in"), sem("ln2_var"), sem("ln2_sqrt"), sem("xn2_ready")
        xT_done, xT_ready, lg_done, gap_ready, gap_exp = (
            sem("xT_done"), sem("xT_ready"), sem("lg_done"), sem("gap_ready"), sem("gap_exp"))
        wf_ready, wT_done, wT_ready, b2_done, b2_added = (
            sem("wf_ready"), sem("wT_done"), sem("wT_ready"), sem("b2_done"), sem("b2_added"))
        h_done, h_ready, y_done, y_added = sem("h_done"), sem("h_ready"), sem("y_done"), sem("y_added")
        out_ready, out_done, x_used, x2_free = sem("out_ready"), sem("out_done"), sem("x_used"), sem("x2_free")

        adj_v = adj.rearrange("(t p) (k w) -> p t k w", p=P, w=CH * P)
        x_v = x.rearrange("(t p) d -> p t d", p=P)
        h0_v = h0.rearrange("(t p) d -> p t d", p=P)
        out_v = out.rearrange("(t p) d -> p t d", p=P)
        feat_v = feat_dram.rearrange("(t p) d -> p t d", p=P)
        RING = 4
        PAIRS = T // 2
        BP = JB // 2

        FG = (0, JB, T - SB, T)
        QUARTERS = ((0, 0), (0, 1), (1, 0), (1, 1))
        HI_ACT = [3 if 5 < p < 11 else 2 for p in range(PAIRS)]
        FE = 3

        def row(ap, n):
            return ap.rearrange("(o n) -> o n", o=1).to_broadcast([P, n])

        block = ctx.enter_context(nc.Block())

        @block.sync
        def _(sp):
            sp.dma_start(coe[:, 0:5], row(temp, 5)).then_inc(temp_in, 16)
            for g in range(XG):
                sl = slice(g * T // XG, (g + 1) * T // XG)
                sp.dma_start(xn[:, sl], x_v[:, sl]).then_inc(x_in[g], 16)
                if g == 0:
                    with nc.allow_non_contiguous_dma(reason="1 KiB, once"):
                        sp.dma_start(acol[:], a.rearrange("(k f) o -> f (k o)", f=F)).then_inc(a_in, 16)

            def chunk(s, b, c):
                sp.dma_start(adjc[:, c], adj_v[:, ds(s * SB, SB), b * 2 + c, :]).then_inc(adj_in[c], 16)

            def next_chunks(s, b):
                for c in range(2):
                    sp.wait_ge(gt_done, s * (2 * B) + (2 * b + c - 1))
                    sp.wait_ge(gt2_done, s * (2 * B) + (2 * b + c - 1))
                    chunk(s, b, c)

            def thresholds(s):
                sp.dma_start(thr[:, 0, :].rearrange("p (t d) -> p t d", d=P),
                             thr_dram[ds(s * SB, SB), :].unsqueeze(0).to_broadcast([P, SB, P])
                             ).then_inc(thr_in, 16)

            def rows(s):
                sp.wait_ge(feat_out, s * 16 + 16)
                sp.dma_start(xs[:], x_v[:, ds(s * SB, SB), :]).then_inc(xs_in, 16)

            def store_features(s):
                sp.wait_ge(feat_ready, s + 1)
                sp.dma_start(feat_v[:, ds(s * SB, SB), :], xs[:]).then_inc(feat_out, 16)

            def superblock(s, first=False, last=False):
                if not first:
                    next_chunks(s, 0)
                    rows(s - 1)
                next_chunks(s, 1)
                if not last:
                    sp.wait_ge(thr_free, s + 1)
                    thresholds(s + 1)
                next_chunks(s, 2)
                next_chunks(s, 3)
                if not first:
                    store_features(s - 1)

            chunk(0, 0, 0)
            chunk(0, 0, 1)
            sp.wait_ge(f1_copied, 1)
            sp.dma_start(thr_dram, thrT).then_inc(thr_out, 16)
            sp.wait_ge(thr_out, 16)
            thresholds(0)
            sp.sem_inc(feat_out, 16)
            superblock(0, first=True)
            with sp.Fori(1, S - 1, 1) as s:
                superblock(s)
            superblock(S - 1, last=True)
            rows(S - 1)
            sp.wait_ge(gt_done, 2 * B * S)
            sp.wait_ge(gt2_done, 2 * B * S)
            sp.wait_ge(code_done, 2 * S * PAIRS)
            for k in range(2):
                sp.dma_start(feats[:, FG[k]:FG[k + 1]], feat_v[:, FG[k]:FG[k + 1]]).then_inc(f_in[k], 16)
            for k in range(2):
                sp.dma_start(w1s[k], W1[k * (E // 2):(k + 1) * (E // 2)].rearrange("e d h -> d e h")).then_inc(w1_in, 16)
            store_features(S - 1)
            sp.wait_ge(feat_out, 16 * S + 16)
            sp.dma_start(feats[:, FG[2]:T], feat_v[:, FG[2]:T]).then_inc(f_in[2], 16)
            sp.wait_ge(v2_done, PAIRS)
            sp.wait_ge(mean_done, 1)
            sp.dma_start(w2s, W2.rearrange("e (k h) d -> h e k d", h=P)).then_inc(weights_in, 16)
            sp.sem_inc(x2_free, 1)
            with sp.Fori(0, S, 1) as s:
                sp.wait_ge(out_ready, s + 1)
                sp.dma_start(out_v[:, ds(s * SB, SB), :], x2[:]).then_inc(out_done, 16)
                sp.wait_ge(out_done, s * 16 + 16)
                sp.sem_inc(x2_free, 1)
            sp.wait_ge(out_done, 16 * S)

        raw = loc[:, 2:6].rearrange("p k t -> p (k t)")
        factors = raw.rearrange("p (t g) -> p t g", g=4)

        @block.gpsimd
        def _(pool):
            nc.gpsimd.memset(identb[:], 0.0)
            nc.gpsimd.memset(ident[:], 0.0)
            nc.gpsimd.memset(meancol[:], 1.0 / N)
            nc.gpsimd.iota(iota[:], [[1, E]], base=0, channel_multiplier=0,
                           allow_small_or_imprecise_dtypes=True)
            pool.drain()
            nc.gpsimd.affine_select(out=identb[:], in_=identb[:], compare_op=ALU.not_equal, fill=1.0,
                                    base=0, pattern=[[-1, P]], channel_multiplier=1)
            nc.gpsimd.affine_select(out=ident[:], in_=ident[:], compare_op=ALU.not_equal, fill=1.0,
                                    base=0, pattern=[[-1, P]], channel_multiplier=1)
            pool.drain().then_inc(const_done, 1)
            pool.dma_start(wrs[:], Wr).then_inc(w_in, 16)
            pool.dma_start(b2s[:], b2).then_inc(w_in, 16)
            pool.dma_start(gb[:, 0:1], gamma.rearrange("(d o) -> d o", o=1)).then_inc(w_in, 16)
            pool.dma_start(gb[:, 1:2], beta.rearrange("(d o) -> d o", o=1)).then_inc(w_in, 16)
            pool.dma_start(brb[:], row(br, E)).then_inc(w_in, 16)
            with nc.allow_non_contiguous_dma(reason="8 KiB of biases, once"):
                pool.dma_start(bcol[:], b1.rearrange("e (k h) -> h e k", h=P)).then_inc(w_in, 16)
            pool.wait_ge(max_ready, 1)
            nc.gpsimd.partition_all_reduce(gmax[:, 1:2], gmax[:, 0:1], P,
                                           bass.bass_isa.ReduceOp.max).then_inc(max_done, 1)
            pool.wait_ge(parts_ready, 1)
            sqv = sq[:].rearrange("p t g (k c) -> p g t k c", k=2)
            nc.gpsimd.tensor_tensor(pf[:, 17:19], pf[:, 15:17], pf[:, 15:17], ALU.mult)
            nc.gpsimd.tensor_scalar(pf[:, 19:21], pf[:, 13:15], QS, None, ALU.mult)
            pool.drain()
            nc.gpsimd.tensor_tensor(pf[:, 17:19], pf[:, 17:19], pf[:, 19:21], ALU.mult)
            pool.drain()
            for c in range(3):
                for k, src in enumerate((pf[:, 15:17], pf[:, 17:19])):
                    nc.gpsimd.tensor_copy(sqv[:, :, :, k, c], src)
                pool.drain()
                if c < 2:
                    for k, src in enumerate((pf[:, 15:17], pf[:, 17:19])):
                        nc.gpsimd.tensor_tensor(src, src, sqv[:, :, :, k, c], ALU.subtract)
                    pool.drain()
            pool.drain().then_inc(squares_ready, 1)
            nc.gpsimd.tensor_copy(wts[:, :, 0], pf[:, 10])
            nc.gpsimd.tensor_copy(wts[:, :, 2], pf[:, 11])
            nc.gpsimd.tensor_tensor(wts[:, :, 1], pf[:, 10], pf[:, 10], ALU.mult)
            nc.gpsimd.tensor_tensor(wts[:, :, 3], pf[:, 11], pf[:, 11], ALU.mult)
            for t in range(1, T, 2):
                hi, lo = v[:, 1, t, 0:F], v[:, 1, t, F:2 * F]
                nc.gpsimd.tensor_scalar(hi, xn[:, t], mant[:, 1, t:t + 1], None, ALU.mult)
                nc.gpsimd.tensor_scalar(quarter, xn[:, t], mant[:, 1, t:t + 1], None, ALU.mult)
                pool.drain()
                nc.gpsimd.tensor_tensor(lo, quarter, hi, ALU.subtract)
                pool.drain().then_inc(quarter_done, 1)

            def softmax_sums(s):
                sl = ds(s * SB, SB)
                nc.gpsimd.tensor_tensor(factors, factors, wts[:, sl, :], ALU.mult)
                pool.drain()
                nc.gpsimd.tensor_tensor(factors[:, :, 0:2], factors[:, :, 0:2], factors[:, :, 2:4], ALU.add)
                pool.drain()
                nc.gpsimd.tensor_scalar(loc[:, 6], factors[:, :, 0], 0.0, None, ALU.is_equal)
                pool.drain()
                nc.gpsimd.tensor_tensor(loc[:, 7], factors[:, :, 0], loc[:, 6], ALU.add)
                pool.drain().then_inc(sums_ready, 1)
                pool.wait_ge(inverse_ready, s + 1)
                nc.gpsimd.tensor_tensor(loc[:, 10], factors[:, :, 1], loc[:, 8], ALU.mult)
                nc.gpsimd.tensor_scalar(loc[:, 9], loc[:, 8], 1.0 / VS, None, ALU.mult)
                nc.gpsimd.tensor_scalar(loc[:, 13], loc[:, 6], 0.5 / N, None, ALU.mult)
                pool.drain()

            def row_scales(s):
                sl = ds(s * SB, SB)
                nc.gpsimd.tensor_tensor(cc[:, sl, 0], loc[:, 9], wts[:, sl, 0], ALU.mult)
                nc.gpsimd.tensor_tensor(cc[:, sl, 1], loc[:, 9], wts[:, sl, 2], ALU.mult)
                nc.gpsimd.tensor_copy(cc[:, sl, 2], loc[:, 6])
                nc.gpsimd.tensor_scalar(loc[:, 11], loc[:, 10], 0.5 / QS, None, ALU.mult)
                pool.drain()
                nc.gpsimd.tensor_tensor(loc[:, 11], loc[:, 11], loc[:, 8], ALU.mult)
                pool.drain()
                nc.gpsimd.tensor_tensor(rs[:, sl], loc[:, 13], loc[:, 11], ALU.add)
                nc.gpsimd.tensor_tensor(loc[:, 12], loc[:, 13], loc[:, 11], ALU.add)
                pool.drain()
                nc.gpsimd.tensor_scalar(loc[:, 13], loc[:, 12], -1.0, coe[:, 7:8], ALU.mult, ALU.add)
                pool.drain()
                nc.gpsimd.tensor_tensor(loc[:, 14], loc[:, 13], rstd[:, sl], ALU.mult)
                pool.drain()
                pool.wait_ge(xs_in, s * 16 + 16)
                nc.gpsimd.tensor_tensor(loc[:, 15], mean[:, sl], loc[:, 14], ALU.mult)
                pool.drain()
                nc.gpsimd.tensor_scalar(loc[:, 15], loc[:, 15], -1.0, None, ALU.mult)
                pool.drain()
                for t in range(SB):
                    nc.gpsimd.tensor_scalar(xs[:, t, :], xs[:, t, :], loc[:, 14, t:t + 1],
                                            loc[:, 15, t:t + 1], ALU.mult, ALU.add)

            def features(s):
                pu, mu = t1[:, :, 0:F], t1[:, :, F:2 * F]
                nc.gpsimd.tensor_tensor(pu, pu, mu, ALU.add)
                pool.drain()
                nc.gpsimd.tensor_tensor(pu, pu, loc[:, 9].unsqueeze(2).to_broadcast([P, SB, F]), ALU.mult)
                nc.gpsimd.tensor_tensor(mu, colmean[:].unsqueeze(1).to_broadcast([P, SB, F]),
                                        loc[:, 6].unsqueeze(2).to_broadcast([P, SB, F]), ALU.mult)
                pool.drain()
                nc.gpsimd.tensor_tensor(xs[:], xs[:], pu, ALU.add)
                pool.drain()
                nc.gpsimd.tensor_tensor(xs[:], xs[:], mu, ALU.add)
                pool.drain()
                nc.gpsimd.tensor_scalar(t1[:, :, 0:F], xs[:], -THRESH, THRESH, ALU.max, ALU.min)
                pool.drain()
                nc.gpsimd.tensor_tensor(xs[:], xs[:], t1[:, :, 0:F], ALU.subtract).then_inc(feat_ready, 1)
                pool.drain().then_inc(rows_done, 1)

            def finish_rows(s):
                pool.wait_ge(combined, s + 1)
                softmax_sums(s)
                row_scales(s)
                features(s)

            with pool.Fori(0, S, 1) as s:
                finish_rows(s)

            pool.wait_ge(bounds_done, 1)
            nc.gpsimd.partition_all_reduce(bound[:, 2:4], bound[:, 0:2], P,
                                           bass.bass_isa.ReduceOp.max).then_inc(bounds_done, 1)

            def rows2(s):
                pool.dma_start(xs[:], x_v[:, ds(s * SB, SB), :]).then_inc(x2_in, 16)
                pool.dma_start(h0s, h0_v[:, ds(s * SB, SB), :]).then_inc(x2_in, 16)
                pool.dma_start(ft, feat_v[:, ds(s * SB, SB), :]).then_inc(x2_in, 16)

            pool.wait_ge(v2_done, PAIRS)
            rows2(0)
            with pool.Fori(1, S, 1) as s:
                pool.wait_ge(v2_done, PAIRS)
                pool.wait_ge(x_used, s)
                rows2(s)

        @block.scalar
        def _(act):
            act.wait_ge(temp_in, 16)
            nc.scalar.activation(coe[:, 5:10], coe[:, 0:5], ACT.Exp, scale=-1.0).then_inc(temp_exp, 1)
            act.wait_ge(ln_done, 1)
            nc.scalar.activation(rstd[:], meanvar[:, :, 1], ACT.Sqrt).then_inc(sq_done, 1)
            act.wait_ge(ln_done, 2)
            for g in range(1, NG, 2):
                for t in range(g * SB, (g + 1) * SB):
                    ins = nc.scalar.activation(xn[:, t], xn[:, t], ACT.Identity, scale=rstd[:, t:t + 1],
                                               bias=nbias[:, t:t + 1])
                ins.then_inc(norm_done[1], 1)
            for g in range(1, NG, 2):
                act.wait_ge(turned, g + 1)
                nc.scalar.activation(xnt[:, g * W:(g + 1) * W], bank[g % 7][:], ACT.Copy).then_inc(copied[1], 1)

            def edge_signs(c, landed):
                act.wait_ge(adj_in[c], landed)
                nc.scalar.activation(natb[:, c, 0:SB - 1], adjc[:, c, 0:SB - 1], ACT.Sign).then_inc(gt_done, 1)

            def positive_masks(s, jt, pair, p, coded=False):
                for q in range(2):
                    if not coded:
                        act.wait_ge(code_done, pair * 2 + (q + 1))
                    act.wait_ge(ring_free, pair * 2 + (q + 1))
                    nc.scalar.activation(ring[:, 0, (2 * p + q) % 4, :],
                                               edges[:, ds((jt + q) * N + s * W, W)], ACT.Relu,
                                               bias=kpow[:, 1, ds(jt + q, 1)], scale=kpow[:, 0, ds(jt + q, 1)]
                                         ).then_inc(pos_ready, 1)

            def evacuate(s, pairs, weights):
                if weights is row_weight:
                    act.wait_ge(rows_done, s + 1)
                act.wait_ge(ring_free, pairs * 2 + RING)
                for t in range(SB):
                    nc.scalar.activation(t1[:, t, :], acc[t][:, 0:2 * F], ACT.Copy,
                                         scale=weights(s, t)).then_inc(evac_done, 1)

            def row_weight(s, t):
                return wts[:, ds(s * SB + t, 1), 0]

            def row_scale(s, t):
                return cc[:, ds(s * SB + t, 1), 0]

            def high_parts(src, jt, parts):
                for t, g in parts:
                    ins = nc.scalar.activation(v[:, g, jt + t, 0:F], src[:, jt + t], ACT.Copy,
                                               scale=mant[:, g, jt + t:jt + t + 1])
                ins.then_inc(hi_done, 1)

            def step(s, b, prev=None, first=False, last=False):
                n = s * B + b
                edge_signs(1, n * 16 + 16)
                for p in range(BP):
                    if p == BP // 2 and not last:
                        edge_signs(0, n * 16 + 32)
                    if first:
                        high_parts(xn, b * JB + 2 * p, QUARTERS[0:3])
                    positive_masks(s, b * JB + 2 * p, n * BP + p, p)
                    if prev is not None and p == 0:
                        evacuate(prev, s * PAIRS, row_weight)

            def superblock(s, first=False, last=False):
                step(s, 0, None if first else s - 1, first=first)
                for b in range(1, B):
                    step(s, b, first=first, last=last and b == B - 1)

            edge_signs(0, 16)
            act.wait_ge(f1_turned, 1)
            nc.scalar.activation(thrT, bank[3][0:T, 0:P], ACT.Copy).then_inc(f1_copied, 1)
            act.wait_ge(exponents_ready, 1)
            nc.scalar.activation(pf[:, 8:12], pf[:, 4:8], ACT.Exp).then_inc(factors_ready, 1)
            act.wait_ge(parts_ready, 1)
            superblock(0, first=True)
            with act.Fori(1, S - 1, 1) as s:
                superblock(s)
            superblock(S - 1, last=True)

            def gelu(s, e):
                for k in range(HH):
                    act.wait_ge(h_done, s * (E * HH) + (e * HH + k + 1))
                    if k == 0:
                        act.wait_ge(y_done, s * E + (e + 1))
                    nc.scalar.activation(hT[e % 2][:, k, :], hb[k][:], ACT.Gelu,
                                         bias=bcol[:, e, k:k + 1],
                                         scale=bound[:, 6:7]).then_inc(h_ready, 1)

            def propagate(s, front, tail):
                for p in range(PAIRS):
                    if tail is not None and p < E - (FE - 1):
                        gelu(tail, FE - 1 + p)
                    if front is not None and p > PAIRS - FE:
                        gelu(front, p - (PAIRS - FE) - 1)
                    if front is None and tail is None:
                        if 2 * p in FG:
                            act.wait_ge(f_in[FG.index(2 * p)], 16)
                        high_parts(feats, 2 * p, QUARTERS[0:HI_ACT[p]])
                    if s is not None:
                        positive_masks(s, 2 * p, (s + S) * PAIRS + p, p, coded=True)
                    if p == 0 and front is None and tail is None:
                        evacuate(S - 1, S * PAIRS, row_weight)
                    if front is None:
                        continue
                    if p == 0:
                        evacuate(front, front * PAIRS + (S + 1) * PAIRS, row_scale)
                    if p == (4 if s is None else 5):
                        act.wait_ge(ln2_var, front + 1)
                        nc.scalar.activation(loc[:, 8, :], loc[:, 7, :], ACT.Sqrt).then_inc(ln2_sqrt, 1)
                    if p == 10:
                        act.wait_ge(gap_ready, front + 1)
                        nc.scalar.activation(small[:, 1, 0:SB], small[:, 0, 0:SB], ACT.Exp).then_inc(gap_exp, 1)

            propagate(0, None, None)
            propagate(1, 0, None)
            with act.Fori(2, S, 1) as s:
                propagate(s, s - 1, s - 2)
            propagate(None, S - 1, S - 2)
            propagate(None, None, S - 1)

        @block.vector
        def _(dve):
            dve.wait_ge(temp_exp, 1)
            nc.vector.tensor_scalar(coe[:, 5:10], coe[:, 5:10], 1.0, None, ALU.add)
            dve.drain()
            nc.vector.reciprocal(coe[:, 0:5], coe[:, 5:10])
            dve.drain()
            nc.vector.tensor_scalar(coe[:, 5:10], coe[:, 0:5], -1.0, 1.0, ALU.mult, ALU.add)
            dve.drain()
            nc.vector.tensor_tensor(coe[:, 10:11], coe[:, 6:7], coe[:, 0:1], ALU.mult)
            nc.vector.tensor_tensor(coe[:, 11:12], coe[:, 6:7], coe[:, 5:6], ALU.mult)
            nc.vector.tensor_scalar(coe[:, 8:9], coe[:, 3:4], -1.0, None, ALU.mult)
            for t in range(T):
                if t % (T // XG) == 0:
                    dve.wait_ge(x_in[t * XG // T], 16)
                nc.vector.bn_stats(stats[:, t], xn[:, t])
            dve.drain()
            for t in range(T):
                nc.vector.bn_aggr(meanvar[:, t], stats[:, t])
            dve.drain()
            nc.vector.tensor_scalar(meanvar[:, :, 1], meanvar[:, :, 1], EPS, None, ALU.add).then_inc(ln_done, 1)
            nc.vector.tensor_copy(mean[:], meanvar[:, :, 0])
            dve.wait_ge(sq_done, 1)
            nc.vector.reciprocal(rstd[:], rstd[:])
            dve.drain()
            nc.vector.scalar_tensor_tensor(nbias, mean[:], -1.0, rstd[:], ALU.mult, ALU.mult)
            dve.drain().then_inc(ln_done, 1)
            for g in range(0, NG, 2):
                for t in range(g * SB, (g + 1) * SB):
                    ins = nc.vector.tensor_scalar(xn[:, t], xn[:, t], mean[:, t:t + 1], rstd[:, t:t + 1],
                                                  ALU.subtract, ALU.mult)
                ins.then_inc(norm_done[0], 1)
            for g in range(0, NG, 2):
                dve.wait_ge(turned, g + 1)
                nc.vector.tensor_copy(xnt[:, g * W:(g + 1) * W], bank[g % 7][:]).then_inc(copied[0], 1)

            def edge_signs(c, landed):
                dve.wait_ge(adj_in[c], landed)
                nc.vector.tensor_scalar(natb[:, c, SB - 1], adjc[:, c, SB - 1], 0.0, None,
                                        ALU.is_gt).then_inc(gt2_done, 1)

            edge_signs(0, 16)
            dve.wait_ge(copied[1], NG // 2)
            dve.drain()
            nc.vector.tensor_reduce(colsum, xnt, X, ALU.add)
            dve.drain()
            nc.vector.tensor_scalar(diag, ident[:], colsum, None, ALU.mult).then_inc(diag_ready, 1)
            dve.wait_ge(f_done, 1)
            nc.vector.tensor_copy(pf[:, 1:3].rearrange("p k t -> p t k"),
                                  bank[7][:, 0:2 * T].rearrange("p (t k) -> p t k", k=2))
            dve.drain()
            nc.vector.tensor_reduce(gmax[:, 0:1], pf[:, 2], X, ALU.max).then_inc(max_ready, 1)
            nc.vector.tensor_scalar(pf[:, 3], pf[:, 1], -1.0, None, ALU.mult).then_inc(f1_ready, 1)
            nc.vector.tensor_copy(f2[:], pf[:, 2])
            dve.wait_ge(max_done, 1)
            nc.vector.tensor_scalar(pf[:, 4], pf[:, 2], gmax[:, 1:2], None, ALU.subtract)
            nc.vector.tensor_scalar(pf[:, 6], pf[:, 1], gmax[:, 1:2], None, ALU.add)
            dve.drain()
            nc.vector.tensor_scalar(pf[:, 5], pf[:, 4], 0.2, HEADROOM, ALU.mult, ALU.add)
            nc.vector.tensor_scalar(pf[:, 7], pf[:, 6], 0.2, None, ALU.mult)
            dve.drain()
            nc.vector.tensor_scalar(pf[:, 4], pf[:, 4], HEADROOM, None, ALU.add)
            nc.vector.tensor_tensor(pf[:, 12], pf[:, 6], pf[:, 7], ALU.max)
            dve.drain()
            nc.vector.tensor_tensor(pf[:, 6], pf[:, 6], pf[:, 12], ALU.subtract)
            nc.vector.tensor_tensor(pf[:, 7], pf[:, 7], pf[:, 12], ALU.subtract)
            dve.drain().then_inc(exponents_ready, 1)
            dve.wait_ge(factors_ready, 1)
            fac = pf[:, 8:10].bitcast(U32)
            nc.vector.tensor_scalar(pf[:, 13:15].bitcast(U32), fac, 0x7F800000, None, ALU.bitwise_and)
            nc.vector.tensor_scalar(pf[:, 15:17].bitcast(U32), fac, 0x007FFFFF, 0x3F800000,
                                    ALU.bitwise_and, ALU.bitwise_or)
            dve.drain()
            nc.vector.tensor_copy(kpow[:, 0], pf[:, 13])
            nc.vector.tensor_scalar(kpow[:, 1], pf[:, 13], -2.0, None, ALU.mult)
            nc.vector.tensor_copy(kpow[:, 2], pf[:, 14])
            nc.vector.tensor_scalar(mant[:], pf[:, 15:17], VS, None, ALU.mult)
            dve.drain().then_inc(parts_ready, 1)
            dve.wait_ge(colmean_done, 1)
            nc.vector.tensor_copy(colmean[:], bank[7][:, P:P + F])

            def low_parts(src, jt, made, own, others):
                hi, lo = v[:, :, :, 0:F], v[:, :, :, F:2 * F]
                for t, g in own:
                    nc.vector.tensor_scalar(hi[:, g, jt + t], src[:, jt + t], mant[:, g, jt + t:jt + t + 1],
                                            None, ALU.mult)
                dve.wait_ge(hi_done, made)
                for t, g in others + own:
                    if own and (t, g) == own[0]:
                        dve.drain()
                    ins = nc.vector.scalar_tensor_tensor(lo[:, g, jt + t], src[:, jt + t],
                                                         mant[:, g, jt + t:jt + t + 1],
                                                         hi[:, g, jt + t], ALU.mult, ALU.subtract)
                return ins

            def codes(s, b, n, p):
                dve.wait_ge(tp_done, n * BP + (p + 1))
                for q in (2 * p, 2 * p + 1):
                    jt = b * JB + q
                    nc.vector.scalar_tensor_tensor(
                        edges[:, ds(jt * N + s * W, W)], thr[:, 1, :], f2[:, ds(jt, 1)],
                        tp[p % 2][:].bitcast(F16)[:, (q % 2) * W:(q % 2 + 1) * W], ALU.is_lt, ALU.add
                    ).then_inc(code_done, 1)

            def negative_masks(s, jt, pair, p, coded=False):
                for q in range(2):
                    dve.wait_ge(ring_free, pair * 2 + (q + 1))
                    if not coded:
                        dve.wait_ge(code_done, pair * 2 + (q + 1))
                    nc.vector.tensor_scalar(ring[:, 1, (2 * p + q) % 4, :],
                                                  edges[:, ds((jt + q) * N + s * W, W)], 2.0,
                                                  kpow[:, 2, ds(jt + q, 1)], ALU.is_equal, ALU.mult
                                            ).then_inc(neg_ready, 1)

            def combine(s, evacuated, weights):
                for t in range(SB):
                    dve.wait_ge(evac_done, evacuated + (t + 1))
                    nc.vector.scalar_tensor_tensor(t1[:, t, :], acc[t][:, 2 * F:4 * F], weights(s, t),
                                                   t1[:, t, :], ALU.mult, ALU.add).then_inc(acc_free, 1)
                return dve.drain()

            def read_squares(s):
                dve.wait_ge(rows_done, s)
                dve.wait_ge(ring_free, s * (2 * PAIRS) + RING)
                nc.vector.tensor_reduce(raw, sqb[:, 0:SB * 12].rearrange("p (g c) -> p g c", c=3), X, ALU.add)
                dve.drain()

            def invert_sums(s):
                dve.wait_ge(sums_ready, s + 1)
                nc.vector.reciprocal(loc[:, 8], loc[:, 7]).then_inc(inverse_ready, 1)

            def row_weight(s, t):
                return wts[:, ds(s * SB + t, 1), 2]

            def row_scale(s, t):
                return cc[:, ds(s * SB + t, 1), 1]

            def step(s, b, prev=None, first=False, last=False):
                n = s * B + b
                for p in range(BP):
                    if p == 0:
                        edge_signs(1, n * 16 + 16)
                    if p == BP // 2 and not last:
                        edge_signs(0, n * 16 + 32)
                    codes(s, b, n, p)
                    if first:
                        low_parts(xn, b * JB + 2 * p, b * BP + p + 1, (),
                                  QUARTERS[0:3]).then_inc(v_done, 1)
                    if p:
                        negative_masks(s, b * JB + 2 * (p - 1), n * BP + (p - 1), p - 1)
                    if prev is not None and p == 1:
                        read_squares(s)
                        combine(prev, prev * SB, row_weight).then_inc(combined, 1)
                    if prev is not None and p == 2:
                        invert_sums(prev)
                negative_masks(s, b * JB + 2 * (BP - 1), n * BP + (BP - 1), BP - 1)

            def superblock(s, first=False, last=False):
                dve.wait_ge(thr_in, s * 16 + 16)
                nc.vector.tensor_copy(thr[:, 1, :], thr[:, 0, :])
                dve.drain().then_inc(thr_free, 1)
                step(s, 0, None if first else s - 1, first=first)
                if first:
                    for b in range(1, B):
                        step(s, b, first=True)
                    return
                with dve.Fori(1, B - 1 if last else B, 1) as b:
                    step(s, b)
                if last:
                    step(s, B - 1, last=True)

            superblock(0, first=True)
            with dve.Fori(1, S - 1, 1) as s:
                superblock(s)
            superblock(S - 1, last=True)
            dve.wait_ge(w_in, 96)

            def weight_bounds(k):
                dve.wait_ge(w1_in, 32)
                part = w1s[k // 2].rearrange("p e h -> p (e h)")
                nc.vector.tensor_reduce(loc[:, k % 2, k // 2:k // 2 + 1], part, X, (ALU.max, ALU.min)[k % 2])

            def bounds():
                dve.wait_ge(w_in, 96)
                dve.drain()
                nc.vector.tensor_scalar(loc[:, 1, 0:2], loc[:, 1, 0:2], -1.0, None, ALU.mult)
                nc.vector.tensor_scalar(loc[:, 0, 2:4], gb[:], -1.0, None, ALU.mult)
                dve.drain()
                nc.vector.tensor_tensor(loc[:, 0, 0:2], loc[:, 0, 0:2], loc[:, 1, 0:2], ALU.max)
                nc.vector.tensor_tensor(loc[:, 0, 2:4], loc[:, 0, 2:4], gb[:], ALU.max)
                dve.drain()
                nc.vector.tensor_tensor(bound[:, 0:1], loc[:, 0, 0:1], loc[:, 0, 1:2], ALU.max)
                nc.vector.scalar_tensor_tensor(bound[:, 1:2], loc[:, 0, 2:3], 12.0, loc[:, 0, 3:4],
                                               ALU.mult, ALU.add).then_inc(bounds_done, 1)

            def scales():
                dve.wait_ge(bounds_done, 2)
                nc.vector.tensor_scalar(bound[:, 2:4], bound[:, 2:4], 1e-18, None, ALU.max)
                dve.drain()
                nc.vector.tensor_scalar(bound[:, 4:6].bitcast(U32), bound[:, 2:4].bitcast(U32), 0x7F800000, None,
                                        ALU.bitwise_and)
                dve.drain()
                nc.vector.tensor_scalar(bound[:, 4:6], bound[:, 4:6], 2.0 ** -13, None, ALU.mult)
                dve.drain()
                nc.vector.reciprocal(bound[:, 2:4], bound[:, 4:6])
                nc.vector.tensor_tensor(bound[:, 6:7], bound[:, 4:5], bound[:, 5:6], ALU.mult)
                dve.drain()

            def split_weights(q):
                src = w1s[q // 2][:, q % 2 * 2:q % 2 * 2 + 2]
                hi, lo = w1[:, 0, 2 * q:2 * q + 2], w1[:, 1, 2 * q:2 * q + 2]
                nc.vector.tensor_scalar(hi, src, bound[:, 2:3], None, ALU.mult)
                dve.drain()
                nc.vector.scalar_tensor_tensor(lo, src, bound[:, 2:3], hi, ALU.mult,
                                               ALU.subtract).then_inc(w1_split, 1)

            def split_columns():
                dve.drain()
                nc.vector.tensor_scalar(z[:, 0], xnT, bound[:, 3:4], None, ALU.mult)
                dve.drain()
                nc.vector.scalar_tensor_tensor(z[:, 1], xnT, bound[:, 3:4], z[:, 0], ALU.mult,
                                               ALU.subtract).then_inc(z_ready, 1)

            def attended(s):
                sl = ds(s * SB, SB)
                nc.vector.tensor_copy(loc[:, 6], cc[:, sl, 2])
                nc.vector.tensor_scalar(loc[:, 2], rs[:, sl], coe[:, 1:2], coe[:, 10:11], ALU.mult, ALU.add)
                nc.vector.tensor_tensor(t1[:, :, 0:F], t1[:, :, 0:F], t1[:, :, F:2 * F], ALU.add)
                dve.drain()
                for t in range(SB):
                    nc.vector.scalar_tensor_tensor(t1[:, t, 0:F], colmean[:], loc[:, 6, t:t + 1],
                                                   t1[:, t, 0:F], ALU.mult, ALU.add)
                dve.drain()
                dve.wait_ge(x2_in, s * 48 + 48)

            def layer_rows(s):
                pu = t1[:, :, 0:F]
                nc.vector.scalar_tensor_tensor(ft, pu, coe[:, 8:9], ft, ALU.mult, ALU.add)
                nc.vector.scalar_tensor_tensor(xs[:], pu, coe[:, 1:2], xs[:], ALU.mult, ALU.add)
                dve.drain()
                nc.vector.scalar_tensor_tensor(xs[:], h0s, coe[:, 11:12], xs[:], ALU.mult, ALU.add)
                dve.drain()
                for t in range(SB):
                    nc.vector.scalar_tensor_tensor(xs[:, t, :], ft[:, t, :], loc[:, 2, t:t + 1], xs[:, t, :],
                                                   ALU.mult, ALU.add)
                dve.drain()

            def norm_stats():
                for t in range(SB):
                    nc.vector.bn_stats(small[:, 2 + t, 0:6], xs[:, t, :])
                dve.drain()
                for t in range(SB):
                    nc.vector.bn_aggr(loc[:, 9:11, t], small[:, 2 + t, 0:6])
                dve.drain()
                nc.vector.tensor_scalar(loc[:, 11], loc[:, 10], EPS, EPS, ALU.add, ALU.mult)
                dve.drain()
                nc.vector.tensor_tensor(loc[:, 7], loc[:, 11], loc[:, 10], ALU.add).then_inc(ln2_var, 1)

            def norm_rows(s):
                dve.wait_ge(ln2_sqrt, s + 1)
                nc.vector.reciprocal(loc[:, 12], loc[:, 8])
                dve.drain()
                for t in range(SB):
                    ins = nc.vector.tensor_scalar(t1[:, t, 0:F], xs[:, t, :], loc[:, 9, t:t + 1],
                                                  loc[:, 12, t:t + 1], ALU.subtract, ALU.mult)
                ins.then_inc(xn2_ready, 1)

            def norm_columns(s):
                dve.wait_ge(xT_done, s + 1)
                nc.vector.tensor_scalar(xnT, hb[0][:], gb[:, 0:1], gb[:, 1:2], ALU.mult, ALU.add).then_inc(xT_ready, 1)

            def two_largest(s):
                dve.wait_ge(lg_done, s + 1)
                nc.vector.tensor_tensor(lg[:], hb[1][:, 0:SB * E].rearrange("p (t e) -> p t e", e=E),
                                        brb[:].unsqueeze(1).to_broadcast([P, SB, E]), ALU.add)
                dve.drain()
                for t in range(SB):
                    nc.vector.max(top[:, t, :], lg[:, t, :])
                dve.drain()
                for t in range(SB):
                    nc.vector.max_index(tix[:, t, :], top[:, t, :], lg[:, t, :])
                nc.vector.tensor_tensor(small[:, 0, 0:SB], top[:, :, 1], top[:, :, 0], ALU.subtract).then_inc(gap_ready, 1)
                dve.drain()
                nc.vector.tensor_copy(top[:, :, 2:4], tix[:, :, 0:2])

            def expert_weights(s):
                dve.wait_ge(gap_exp, s + 1)
                nc.vector.tensor_scalar(loc[:, 13], small[:, 1, 0:SB], 1.0, None, ALU.add)
                dve.drain()
                nc.vector.reciprocal(loc[:, 14], loc[:, 13])
                dve.drain()
                nc.vector.tensor_tensor(loc[:, 15], loc[:, 14], small[:, 1, 0:SB], ALU.mult)
                dve.drain()
                for t in range(SB):
                    for k in range(2):
                        nc.vector.tensor_scalar(wf[:, k, t, :], iota[:], top[:, t, 2 + k:3 + k],
                                                loc[:, 14 + k, t:t + 1], ALU.is_equal, ALU.mult)
                dve.drain()
                nc.vector.tensor_tensor(wf[:, 0], wf[:, 0], wf[:, 1], ALU.add).then_inc(wf_ready, 1)

            def expert_biases(s):
                dve.wait_ge(wT_done, s + 1)
                nc.vector.tensor_copy(wT, yb[1][0:E, :]).then_inc(wT_ready, 1)
                dve.wait_ge(b2_done, s + 1)
                dve.wait_ge(x2_free, s + 1)
                nc.vector.tensor_tensor(x2[:], xs[:], yb[0][:].rearrange("p (t d) -> p t d", d=F), ALU.add).then_inc(b2_added, 1)
                dve.drain().then_inc(x_used, 1)

            def add_expert(s, e):
                dve.wait_ge(y_done, s * E + (e + 3))
                if e == 0:
                    dve.wait_ge(b2_added, s + 1)
                else:
                    dve.wait_ge(y_added, s * E + (e + 1))
                for t in range(SB):
                    ins = nc.vector.scalar_tensor_tensor(
                        x2[:, t, :], yb[(e + 1) % 2][:, t * F:(t + 1) * F], wf[:, 0, t, e:e + 1],
                        x2[:, t, :], ALU.mult, ALU.add)
                ins.then_inc(y_added, 1)

            def propagate(s, front, tail):
                for p in range(PAIRS):
                    if front is None and tail is None:
                        if 2 * p in FG:
                            dve.wait_ge(f_in[FG.index(2 * p)], 16)
                        low_parts(feats, 2 * p, PAIRS + p + 1, QUARTERS[HI_ACT[p]:],
                                  QUARTERS[0:HI_ACT[p]]).then_inc(v2_done, 1)
                        if p == 2:
                            invert_sums(S - 1)
                        if p >= 6 and p < 10:
                            weight_bounds(p - 6)
                        if p == 10:
                            bounds()
                    if s is not None:
                        negative_masks(s, 2 * p, (s + S) * PAIRS + p, p, coded=True)
                    if p == 0 and front is None and tail is None:
                        read_squares(S)
                        combine(S - 1, (S - 1) * SB, row_weight).then_inc(combined, 1)
                    if tail is not None and p < E - (FE - 2):
                        add_expert(tail, FE - 2 + p)
                        if FE - 2 + p == E - 1:
                            dve.drain().then_inc(out_ready, 1)
                    if front is None:
                        continue
                    if p == 0:
                        combine(front, (front + S) * SB, row_scale)
                    if p == 1 and tail is None:
                        dve.wait_ge(mean_done, 1)
                        nc.vector.tensor_copy(colmean[:], bank[7][:, 0:F])
                        scales()
                    if p == (1 if s is None else 2):
                        attended(front)
                    if p == (2 if s is None else 3):
                        layer_rows(front)
                    if p == (3 if s is None else 4):
                        norm_stats()
                    if p == (4 if s is None else 5):
                        norm_rows(front)
                    if tail is None and p in (6, 8, 10, 11):
                        split_weights((6, 8, 10, 11).index(p))
                    if p == 7:
                        norm_columns(front)
                    if p == 8:
                        split_columns()
                    if p == 9:
                        two_largest(front)
                    if p == 10:
                        expert_weights(front)
                    if p == 12:
                        expert_biases(front)
                    if p > PAIRS - FE + 1:
                        add_expert(front, p - (PAIRS - FE + 2))

            propagate(0, None, None)
            propagate(1, 0, None)
            with dve.Fori(2, S, 1) as s:
                propagate(s, s - 1, s - 2)
            propagate(None, S - 1, S - 2)
            propagate(None, None, S - 1)

        @block.tensor
        def _(pe):
            pe.sem_inc(ring_free, RING)
            pe.sem_inc(acc_free, SB)
            pe.sem_inc(rows_done, 1)
            pe.wait_ge(const_done, 1)
            for g in range(NG):
                pe.wait_ge(norm_done[g % 2], g // 2 + 1)
                if g >= 7:
                    pe.wait_ge(copied[(g - 7) % 2], (g - 7) // 2 + 1)
                for t in range(SB):
                    tr = nc.tensor.transpose(bank[g % 7][:, t * P:(t + 1) * P], xn[:, g * SB + t], ident[:])
                tr.then_inc(turned, 1)
            pe.wait_ge(a_in, 16)
            for t in range(T):
                g = t // SB
                if t % SB == 0:
                    pe.wait_ge(copied[g % 2], g // 2 + 1)
                mm = nc.tensor.matmul(bank[7][:, 2 * t:2 * t + 2], xnt[:, t * P:(t + 1) * P], acol[:],
                                      start=True, stop=True)
            mm.then_inc(f_done, 1)

            def turn(p, chunks):
                pe.wait_ge(gt_done, chunks)
                pe.wait_ge(gt2_done, chunks)
                for q in range(2):
                    for t in range(SB):
                        k = (2 * p + q) % CH
                        tr = nc.tensor.transpose(
                            tp[p % 2][:].bitcast(BF16)[:, q * W + t * P:q * W + (t + 1) * P],
                            natb[:, (p * 2) // CH % 2, t, k * P:(k + 1) * P], identb[:])
                tr.then_inc(tp_done, 1)

            def sums(s, jt, pair, p, first, squares, before=0):
                for q in range(2):
                    pe.wait_ge(pos_ready, pair * 2 + (q + 1))
                    pe.wait_ge(neg_ready, pair * 2 + (q + 1))
                    lead = first and q == 0
                    for t in range(SB):
                        if lead:
                            pe.wait_ge(acc_free, s * SB + (before * SB + t + 1))
                        for g in range(2):
                            lhs = ring[:, g, (2 * p + q) % 4, t * P:(t + 1) * P]
                            mm = nc.tensor.matmul(acc[t][:, g * 2 * F:(g + 1) * 2 * F], lhs, v[:, g, ds(jt + q, 1), :],
                                                  start=lead and g == 0, stop=False, skip_group_check=True)
                            if squares:
                                o = (t * 2 + g) * 6
                                mm = nc.tensor.matmul(sqb[:, o:o + 6], lhs, sq[:, ds(jt + q, 1), g, :],
                                                      start=lead and g == 0 and t == 0, stop=False,
                                                      skip_group_check=True)
                    mm.then_inc(ring_free, 1)

            def step(s, b, first=False, last=False):
                n = s * B + b
                for p in range(BP):
                    if p < BP - 2 or not last:
                        pe.wait_ge(code_done, (n * BP + p) * 2 + 2)
                        turn((p + 2) % BP, n * 2 + ((p + 2) // 2 + 1))
                    pe.wait_ge(v_done, b * BP + p + 1)
                    pe.wait_ge(quarter_done, b * BP + p + 1)
                    sums(s, b * JB + 2 * p, n * BP + p, p, first and p == 0, True)

            def superblock(s, last=False):
                step(s, 0, first=True)
                with pe.Fori(1, B - 1 if last else B, 1) as b:
                    step(s, b)
                if last:
                    step(s, B - 1, last=True)

            turn(0, 1)
            turn(1, 1)
            pe.wait_ge(f1_ready, 1)
            nc.tensor.transpose(bank[3][0:T, 0:P], pf[:, 3], ident[:]).then_inc(f1_turned, 1)
            pe.wait_ge(diag_ready, 1)
            nc.tensor.matmul(bank[7][:, P:P + F], meancol[:].to_broadcast([P, P]), diag,
                             start=True, stop=True).then_inc(colmean_done, 1)
            pe.wait_ge(squares_ready, 1)
            with pe.Fori(0, S - 1, 1) as s:
                superblock(s)
            superblock(S - 1, last=True)

            pe.sem_inc(y_done, 2)
            pe.sem_inc(y_added, 1)

            def rows_to_columns(s):
                pe.wait_ge(xn2_ready, s + 1)
                for t in range(SB):
                    tr = nc.tensor.transpose(hb[0][:, t * P:(t + 1) * P], t1[:, t, 0:F], ident[:])
                tr.then_inc(xT_done, 1)

            def logits(s):
                pe.wait_ge(xT_ready, s + 1)
                for t in range(SB):
                    mm = nc.tensor.matmul(hb[1][:, t * E:(t + 1) * E], xnT[:, t * P:(t + 1) * P], wrs[:],
                                          start=True, stop=True)
                mm.then_inc(lg_done, 1)

            def weights_to_columns(s):
                pe.wait_ge(wf_ready, s + 1)
                pe.wait_ge(y_added, s * E + 1)
                for t in range(SB):
                    tr = nc.tensor.transpose(yb[1][0:E, t * P:(t + 1) * P], wf[:, 0, t, :], ident[:])
                tr.then_inc(wT_done, 1)

            def expert_biases(s):
                pe.wait_ge(wT_ready, s + 1)
                for t in range(SB):
                    mm = nc.tensor.matmul(yb[0][:, t * F:(t + 1) * F], wT[:, t * P:(t + 1) * P], b2s[:],
                                          start=True, stop=True)
                mm.then_inc(b2_done, 1)

            def hidden(s, e):
                for k in range(HH):
                    if e < 2 and k == 0:
                        pe.wait_ge(w1_split, 2 * e + 2)
                        pe.wait_ge(weights_in, 16)
                    if e == 0 and k == 0:
                        pe.wait_ge(z_ready, s + 1)
                    if e == 0 and k:
                        pe.wait_ge(gap_ready, s + 1)
                    if e:
                        pe.wait_ge(h_ready, s * (E * HH) + (e * HH + k - 1))
                    for i, j in ((0, 0), (0, 1), (1, 0)):
                        mm = nc.tensor.matmul(hb[k][:], w1[:, i, e, k * P:(k + 1) * P], z[:, j],
                                              start=(i + j == 0), stop=(i == 1))
                    mm.then_inc(h_done, 1)

            def expert_rows(s, e):
                pe.wait_ge(h_ready, s * (E * HH) + (e * HH + 2))
                pe.wait_ge(y_added, s * E + max(e, 1))
                if e == 1:
                    pe.wait_ge(b2_added, s + 1)
                for t in range(SB):
                    for k in range(HH):
                        mm = nc.tensor.matmul(yb[(e + 1) % 2][:, t * F:(t + 1) * F],
                                              hT[e % 2][:, k, t * P:(t + 1) * P], w2s[:, e, k, :],
                                              start=(k == 0), stop=(k == HH - 1))
                mm.then_inc(y_done, 1)

            def propagate(s, front, tail):
                for p in range(PAIRS):
                    if s is not None:
                        if front is None:
                            pe.wait_ge(v2_done, p + 1)
                        sums(s, 2 * p, (s + S) * PAIRS + p, p, p == 0, False, S)
                        if front is None:
                            for t in (2 * p, 2 * p + 1):
                                mm = nc.tensor.matmul(bank[7][:, 0:F], meancol[:].to_broadcast([P, P]), feats[:, t],
                                                      start=(t == 0), stop=(t == T - 1))
                            if p == PAIRS - 1:
                                mm.then_inc(mean_done, 1)
                    if tail is not None and p < E - FE:
                        if FE + p + 1 < E:
                            hidden(tail, FE + p + 1)
                        expert_rows(tail, FE + p)
                    if front is None:
                        continue
                    if p == 5:
                        rows_to_columns(front)
                    if p == 7:
                        logits(front)
                    if p == 9:
                        hidden(front, 0)
                    if p == 10:
                        weights_to_columns(front)
                    if p == 11:
                        expert_biases(front)
                    if p >= PAIRS - FE:
                        hidden(front, p - (PAIRS - FE) + 1)
                        expert_rows(front, p - (PAIRS - FE))

            pe.wait_ge(w_in, 96)
            propagate(0, None, None)
            propagate(1, 0, None)
            with pe.Fori(2, S, 1) as s:
                propagate(s, s - 1, s - 2)
            propagate(None, S - 1, S - 2)
            propagate(None, None, S - 1)


_INS = ["x", "adj", "L0_gnn_h0", "L0_gnn_a", "L0_gnn_temp", "L0_ffn_gamma", "L0_ffn_beta", "L0_ffn_Wr",
        "L0_ffn_br", "L0_ffn_W1", "L0_ffn_b1", "L0_ffn_W2", "L0_ffn_b2"]


def kernel(**inputs):
    import numpy as _np
    import concourse.bacc as _bacc
    from concourse import mybir as _mybir
    from concourse.bass_utils import run_bass_kernel_spmd as _run

    nc = _bacc.Bacc("TRN2", target_bir_lowering=False, num_devices=1, dynamic_dma_scratch_size=8192)
    arrays, args = {}, []
    for name in _INS:
        arr = _np.ascontiguousarray(inputs[name])
        arrays[f"in_{name}"] = arr
        args.append(nc.dram_tensor(f"in_{name}", arr.shape, _mybir.dt.from_np(arr.dtype), kind="ExternalInput").ap())
    args.append(nc.dram_tensor("out_x", (N, F), F32, kind="ExternalOutput").ap())
    program(nc, *args)
    r = _run(nc, [arrays], core_ids=[0])
    return r.results[0]["out_x"]
```
